# Optimizing a Trainium2 kernel written in Bass

```python
import numpy as np
import jax
import jax.numpy as jnp

def _softmax(x, axis=-1):
    return jax.nn.softmax(x, axis=axis)

def _gelu(x):
    return jax.nn.gelu(x, approximate=True)

def _silu(x):
    return jax.nn.silu(x)

def _sigmoid(x):
    return jax.nn.sigmoid(x)

def _layernorm(x, axis=-1, eps=1e-05):
    m = jnp.mean(x, axis=axis, keepdims=True)
    v = jnp.var(x, axis=axis, keepdims=True)
    return (x - m) / jnp.sqrt(v + eps)

def _scatter_add(tgt, idx, src, axis=0):
    return tgt.at[idx].add(src)

def _segment_sum(src, seg, n):
    return jax.ops.segment_sum(src, seg, n)
kernel_name = 'mk_conv_preact_d2_conv_nhwc256_r2_d50e73'

def setup_inputs(seed: int=0):
    np.random.seed(seed)
    _w = jnp.asarray

    def _rec_inputs():
        import jax
        import jax.numpy as jnp
        _gk = jax.random.key(seed)
        x = -8.268e-05 + 0.9999 * jax.random.normal(jax.random.fold_in(_gk, 1), (32, 56, 56, 128), jnp.float32)
        return x
    x = _rec_inputs()

    def _L0_conv_setup():
        import jax, jax.numpy as jnp
        import numpy as np
        WIN = (7, 7)
        SHIFT = (3, 3)
        HEADS = 8

        def _rel_pos_index(wh, ww):
            ch, cw = np.meshgrid(np.arange(wh), np.arange(ww), indexing='ij')
            coords = np.stack([ch, cw]).reshape(2, -1)
            rel = (coords[:, :, None] - coords[:, None, :]).transpose(1, 2, 0)
            rel[:, :, 0] += wh - 1
            rel[:, :, 1] += ww - 1
            rel[:, :, 0] *= 2 * ww - 1
            return rel.sum(-1)

        def _attn_mask(pad_H, pad_W, ws, ss):
            m = np.zeros((pad_H, pad_W))
            h_slices = ((0, -ws[0]), (-ws[0], -ss[0]), (-ss[0], None))
            w_slices = ((0, -ws[1]), (-ws[1], -ss[1]), (-ss[1], None))
            cnt = 0
            for h in h_slices:
                for w in w_slices:
                    m[h[0]:h[1], w[0]:w[1]] = cnt
                    cnt += 1
            m = m.reshape(pad_H // ws[0], ws[0], pad_W // ws[1], ws[1])
            m = m.transpose(0, 2, 1, 3).reshape(-1, ws[0] * ws[1])
            diff = m[:, None, :] - m[:, :, None]
            return np.where(diff != 0, -100.0, 0.0).astype(np.float32)
        key = jax.random.key(seed)
        ks = jax.random.split(key, 6)
        B, H, W, C = (32, 56, 56, 128)
        return {'x': jax.random.normal(ks[0], (B, H, W, C), jnp.float32), 'qkv_weight': jax.random.normal(ks[1], (3 * C, C), jnp.float32) * 0.02, 'qkv_bias': jax.random.normal(ks[2], (3 * C,), jnp.float32) * 0.02, 'proj_weight': jax.random.normal(ks[3], (C, C), jnp.float32) * 0.02, 'proj_bias': jax.random.normal(ks[4], (C,), jnp.float32) * 0.02, 'rel_pos_table': jax.random.normal(ks[5], ((2 * WIN[0] - 1) * (2 * WIN[1] - 1), HEADS), jnp.float32) * 0.02}
    _L0_conv_all = _L0_conv_setup()
    _L0_conv_in = {k: v for k, v in _L0_conv_all.items() if k in ('qkv_weight', 'qkv_bias', 'proj_weight', 'proj_bias', 'rel_pos_table')}
    del _L0_conv_all

    def _L1_conv_setup():
        import jax, jax.numpy as jnp
        import numpy as np
        K_SIZE = 3
        CH_IN = 128
        NFILT = 128

        def _magnitude_aware_weight(w):
            scale = jax.lax.stop_gradient(jnp.mean(jnp.abs(w), axis=(0, 1, 2), keepdims=True))
            bw_no_grad = scale * jnp.sign(w)
            clipped = jnp.clip(w, -1.0, 1.0)
            return jax.lax.stop_gradient(bw_no_grad) - jax.lax.stop_gradient(clipped) + clipped
        key = jax.random.key(seed)
        k1, k2 = jax.random.split(key)
        x = jax.random.normal(k1, (32, 56, 56, CH_IN), dtype=jnp.float32)
        stdv = 1.0 / np.sqrt(K_SIZE * K_SIZE * CH_IN)
        w = jax.random.normal(k2, (K_SIZE, K_SIZE, CH_IN, NFILT), dtype=jnp.float32) * stdv
        pruning_mask = jnp.ones((K_SIZE * K_SIZE * CH_IN, NFILT), dtype=jnp.float32)
        return {'x': x, 'w': w, 'pruning_mask': pruning_mask}
    _L1_conv_all = _L1_conv_setup()
    _L1_conv_in = {k: v for k, v in _L1_conv_all.items() if k in ('w', 'pruning_mask')}
    del _L1_conv_all
    return {'x': x, 'L0_conv_qkv_weight': _L0_conv_in['qkv_weight'], 'L0_conv_qkv_bias': _L0_conv_in['qkv_bias'], 'L0_conv_proj_weight': _L0_conv_in['proj_weight'], 'L0_conv_proj_bias': _L0_conv_in['proj_bias'], 'L0_conv_rel_pos_table': _L0_conv_in['rel_pos_table'], 'L1_conv_w': _L1_conv_in['w'], 'L1_conv_pruning_mask': _L1_conv_in['pruning_mask']}

def reference(x, L0_conv_qkv_weight, L0_conv_qkv_bias, L0_conv_proj_weight, L0_conv_proj_bias, L0_conv_rel_pos_table, L1_conv_w, L1_conv_pruning_mask):
    import jax
    import jax.numpy as jnp

    def _L0_conv_ref(x, qkv_weight, qkv_bias, proj_weight, proj_bias, rel_pos_table):
        import jax, jax.numpy as jnp
        import numpy as np
        WIN = (7, 7)
        SHIFT = (3, 3)
        HEADS = 8

        def _rel_pos_index(wh, ww):
            ch, cw = np.meshgrid(np.arange(wh), np.arange(ww), indexing='ij')
            coords = np.stack([ch, cw]).reshape(2, -1)
            rel = (coords[:, :, None] - coords[:, None, :]).transpose(1, 2, 0)
            rel[:, :, 0] += wh - 1
            rel[:, :, 1] += ww - 1
            rel[:, :, 0] *= 2 * ww - 1
            return rel.sum(-1)

        def _attn_mask(pad_H, pad_W, ws, ss):
            m = np.zeros((pad_H, pad_W))
            h_slices = ((0, -ws[0]), (-ws[0], -ss[0]), (-ss[0], None))
            w_slices = ((0, -ws[1]), (-ws[1], -ss[1]), (-ss[1], None))
            cnt = 0
            for h in h_slices:
                for w in w_slices:
                    m[h[0]:h[1], w[0]:w[1]] = cnt
                    cnt += 1
            m = m.reshape(pad_H // ws[0], ws[0], pad_W // ws[1], ws[1])
            m = m.transpose(0, 2, 1, 3).reshape(-1, ws[0] * ws[1])
            diff = m[:, None, :] - m[:, :, None]
            return np.where(diff != 0, -100.0, 0.0).astype(np.float32)
        B, H, W, C = x.shape
        ws, ss = (list(WIN), list(SHIFT))
        for i in range(2):
            if (H, W)[i] <= ws[i]:
                ws[i] = (H, W)[i]
                ss[i] = 0
        hd = C // HEADS
        pad_b = (ws[0] - H % ws[0]) % ws[0]
        pad_r = (ws[1] - W % ws[1]) % ws[1]
        x = jnp.pad(x, ((0, 0), (0, pad_b), (0, pad_r), (0, 0)))
        pad_H, pad_W = (H + pad_b, W + pad_r)
        shifted = ss[0] + ss[1] > 0
        if shifted:
            x = jnp.roll(x, (-ss[0], -ss[1]), axis=(1, 2))
        nWh, nWw = (pad_H // ws[0], pad_W // ws[1])
        nW, N = (nWh * nWw, ws[0] * ws[1])
        x = x.reshape(B, nWh, ws[0], nWw, ws[1], C).transpose(0, 1, 3, 2, 4, 5).reshape(B * nW, N, C)
        qkv = x @ qkv_weight.T + qkv_bias
        qkv = qkv.reshape(B * nW, N, 3, HEADS, hd).transpose(2, 0, 3, 1, 4)
        q, k, v = (qkv[0], qkv[1], qkv[2])
        q = q * hd ** (-0.5)
        attn = jnp.einsum('whnd,whmd->whnm', q, k)
        rpb = rel_pos_table[np.asarray(_rel_pos_index(ws[0], ws[1]))]
        attn = attn + jnp.transpose(rpb, (2, 0, 1))[None]
        if shifted:
            mask = jnp.asarray(_attn_mask(pad_H, pad_W, ws, ss))
            attn = attn.reshape(B, nW, HEADS, N, N) + mask[None, :, None]
            attn = attn.reshape(B * nW, HEADS, N, N)
        attn = jax.nn.softmax(attn, axis=-1)
        x = jnp.einsum('whnm,whmd->whnd', attn, v).transpose(0, 2, 1, 3).reshape(B * nW, N, C)
        x = x @ proj_weight.T + proj_bias
        x = x.reshape(B, nWh, nWw, ws[0], ws[1], C).transpose(0, 1, 3, 2, 4, 5).reshape(B, pad_H, pad_W, C)
        if shifted:
            x = jnp.roll(x, (ss[0], ss[1]), axis=(1, 2))
        return x[:, :H, :W, :]

    def _L1_conv_ref(x, w, pruning_mask):
        import jax, jax.numpy as jnp
        import numpy as np
        K_SIZE = 3
        CH_IN = 128
        NFILT = 128

        def _magnitude_aware_weight(w):
            scale = jax.lax.stop_gradient(jnp.mean(jnp.abs(w), axis=(0, 1, 2), keepdims=True))
            bw_no_grad = scale * jnp.sign(w)
            clipped = jnp.clip(w, -1.0, 1.0)
            return jax.lax.stop_gradient(bw_no_grad) - jax.lax.stop_gradient(clipped) + clipped
        kernel = _magnitude_aware_weight(w) * pruning_mask.reshape(K_SIZE, K_SIZE, CH_IN, NFILT)
        out = jax.lax.conv_general_dilated(x, kernel, window_strides=(1, 1), padding='SAME', dimension_numbers=('NHWC', 'HWIO', 'NHWC'))
        return out

    def _gn(v, G=32, eps=1e-05):
        B_, H_, W_, C_ = v.shape
        g = v.reshape(B_, H_, W_, G, C_ // G)
        m = jnp.mean(g, axis=(1, 2, 4), keepdims=True)
        s = jnp.var(g, axis=(1, 2, 4), keepdims=True)
        return ((g - m) / jnp.sqrt(s + eps)).reshape(v.shape)

    def _ln_c(v, eps=1e-06):
        m = jnp.mean(v, axis=-1, keepdims=True)
        s = jnp.var(v, axis=-1, keepdims=True)
        return (v - m) / jnp.sqrt(s + eps)

    def _ln_t(v, eps=1e-05):
        m = jnp.mean(v, axis=-1, keepdims=True)
        s = jnp.var(v, axis=-1, keepdims=True)
        return (v - m) / jnp.sqrt(s + eps)

    def _to_tokens(v):
        B_, H_, W_, C_ = v.shape
        return v.reshape(B_, H_ * W_, C_)

    def _from_tokens(t, like):
        return t.reshape(like.shape)
    x = x + _L0_conv_ref(_gn(x), L0_conv_qkv_weight, L0_conv_qkv_bias, L0_conv_proj_weight, L0_conv_proj_bias, L0_conv_rel_pos_table)
    x = x + _L1_conv_ref(_gn(x), L1_conv_w, L1_conv_pruning_mask)
    return x

_drawn_inputs = setup_inputs


def setup_inputs(seed=0):
    import zlib

    import numpy as np

    out = dict(_drawn_inputs(seed))
    spreads = {}
    factors = {'L0_conv_qkv_weight': 6.827,
     'L0_conv_qkv_bias': 8.0,
     'L0_conv_proj_weight': 6.132,
     'L0_conv_proj_bias': 3.231,
     'L0_conv_rel_pos_table': 8.0}
    for name, (base, spread) in spreads.items():
        noise = np.random.default_rng([zlib.crc32(name.encode()), seed]).standard_normal(out[name].shape)
        drawn = base * np.exp(spread * noise) if base else spread * noise
        out[name] = jnp.asarray(drawn.astype(out[name].dtype))
    for name, factor in factors.items():
        out[name] = (out[name] * factor).astype(out[name].dtype)
    return out
```

```python
from contextlib import ExitStack

import concourse.bass as bass
from concourse import mybir

ALU = mybir.AluOpType
ACT = mybir.ActivationFunctionType
AX = mybir.AxisListType
F32 = mybir.dt.float32
F16 = mybir.dt.float16
I32 = mybir.dt.int32
RMAX = bass.bass_isa.ReduceOp.max

IMGS, H, W, C = 32, 56, 56, 128
WIN, SHIFT, HEADS = 7, 3, 8
N = WIN * WIN
HD = C // HEADS
ROWS = H // WIN
NWIN = W // WIN
WP = NWIN // 2
PAIRS = HEADS // 2
UNITS = ROWS * PAIRS
ODD = 64
QP = ODD + N
RT = WIN * W
VW = 2 * HD + 2
TAPS = 9
TILE_ROWS = 8
TILES = H // TILE_ROWS
TP = TILE_ROWS * W
SUB = 4
SP_ = TP // SUB
PIX = H * W
PAD = W + 2
EPS = 1e-5
TINY = 1e-30
RSQRT_SEED = 0x5F3759DF
NEWTON = 3
WRAP = W - SHIFT

LAG_T, LAG_PV = 2, 3
OT_AT, PROJ_AT = 7, 9
COPY_AT = 6
G2_AT, NORM2_AT = 7, 9
TIN_AT, G1_AT, NORM1_AT = 10, 23, 25
SPLIT_AT = {26: (0, 1, 2), 27: (3, 4, 5), 28: (6, 7)}
CONV_AT, CONV_STEPS = 11, 3
STEADY = 2


def live(i, shift=0):
    return not isinstance(i, int) or 0 <= i + shift < IMGS


def need(eng, sem, value):
    if not isinstance(value, int) or value > 0:
        eng.wait_ge(sem, value)


def misc_jobs(i):
    jobs = []
    for u in range(UNITS):
        for at, kind in ((OT_AT, "ot"), (PROJ_AT, "proj")):
            r, rest = divmod(u - at, PAIRS)
            if rest == 0 and live(i, 0 if r >= 0 else -1):
                jobs.append((u, kind, r % ROWS))
        if u in (G2_AT, G2_AT + 1) and live(i, -1):
            jobs.append((u, "gn2", u - G2_AT))
        if 0 <= u - TIN_AT < 2 * TILES and (u - TIN_AT) % 2 == 0 and live(i, 1):
            jobs.append((u, "tin", (u - TIN_AT) // 2))
        if u in (G1_AT, G1_AT + 1) and live(i, 1):
            jobs.append((u, "gn1", u - G1_AT))
        for k in range(TILES):
            turn, at = divmod(CONV_AT + CONV_STEPS * (k + 1) + 1, UNITS)
            if u == at and live(i, -1 - turn):
                jobs.append((u, "tout", k))
    return jobs


def misc_number(i, kind, index):
    if isinstance(i, int):
        before, order = sum(len(misc_jobs(j)) for j in range(-1, i)), misc_jobs(i)
    else:
        order = misc_jobs(STEADY)
        before = i * len(order) + (sum(len(misc_jobs(j)) for j in range(-1, STEADY)) - STEADY * len(order))
    return before + [job[1:] for job in order].index((kind, index))


def misc_at(i, u):
    return [job[1:] for job in misc_jobs(i if isinstance(i, int) else STEADY) if job[0] == u]


def roll_pieces(rows, row0=0):
    cut = min(max(WRAP - row0, 0), rows)
    for a, b in ((0, cut), (cut, rows)):
        for c, d in ((0, WRAP), (WRAP, W)):
            if b > a:
                yield slice(a, b), slice(c, d), (row0 + a + SHIFT) % H, (c + SHIFT) % W


def build_block(nc, x, wqkv, bqkv, wproj, bproj, table, wconv, prune, ident_d, group_d, parity_d, mask_d, out):
    with ExitStack() as ctx:
        def sb(name, shape, dt=F32):
            return ctx.enter_context(nc.sbuf_tensor(name, shape, dt))

        def pb(name, shape):
            return ctx.enter_context(nc.psum_tensor(name, shape, F32))

        def sem(name):
            return ctx.enter_context(nc.semaphore(name))

        scores_ps = pb("scores_ps", [128, 2, 512])
        probsT_ps = pb("probsT_ps", [128, 512])
        attn_ps = pb("attn_ps", [128, 2, 512])
        conv_ps = pb("conv_ps", [128, 512])
        qkv_ps = pb("qkv_ps", [128, 512])
        misc_ps = pb("misc_ps", [128, 512])

        ident = sb("ident", [128, 128])
        group = sb("group", [128, 128])
        parity = sb("parity", [128, 2])
        w_in = sb("w_in", [128, 4, C])
        b_in = sb("b_in", [128, 4])
        wT_hi = sb("wT_hi", [128, 4, C], F16)
        wT_lo = sb("wT_lo", [128, 4, C], F16)
        w_f = sb("w_f", [128, 4, C])
        w_max = sb("w_max", [128, 4])
        w_inv = sb("w_inv", [128, 4])
        bv2 = sb("bv2", [128, 2])
        q_scale, q_bias = sb("q_scale", [128, 1]), sb("q_bias", [128, 1])
        k_scale, k_bias = sb("k_scale", [128, 2]), sb("k_bias", [128, 2])
        out_bias = sb("out_bias", [128, 1])
        bias = sb("bias", [128, 2, PAIRS, WP, 2, N])
        wc_hi = sb("wc_hi", [128, TAPS, C], F16)
        wc_lo = sb("wc_lo", [128, TAPS, C], F16)
        wc_scale = sb("wc_scale", [128, 1])

        x_in = sb("x_in", [SP_, TILES * SUB, C])
        x_a = sb("x_a", [128, H, W])
        x_b = sb("x_b", [128, H, W])
        x_c = sb("x_c", [128, H, W])
        x_n = sb("x_n", [128, H, W])
        tok_hi = sb("tok_hi", [128, ROWS * NWIN, ODD], F16)
        tok_lo = sb("tok_lo", [128, ROWS * NWIN, ODD], F16)
        pad_hi = sb("pad_hi", [128, PAD, PAD], F16)
        pad_lo = sb("pad_lo", [128, PAD, PAD], F16)
        x_out = sb("x_out", [SP_, TILES * SUB, C])

        q = sb("q", [128, 2, NWIN, N])
        k = sb("k", [128, 2, NWIN, 2, N])
        v = sb("v", [128, 2, NWIN, PAIRS, VW])
        s_sb = sb("s_sb", [128, 4, WP, 2, N])
        s_max = sb("s_max", [128, 4, 2 * WP])
        probs = sb("probs", [128, 2, WP, 2, ODD])
        probsT = sb("probsT", [128, 2, NWIN, N])
        recip = sb("recip", [128, 2, 2 * PAIRS, 2])
        o_sb = sb("o_sb", [128, WP, C])
        oT_hi = sb("oT_hi", [128, WIN, W], F16)
        oT_lo = sb("oT_lo", [128, WIN, W], F16)

        class Norm:

            def __init__(self, name, chunks):
                self.stats = sb(f"{name}_stats", [128, chunks, 6])
                self.mv = sb(f"{name}_mv", [128, 2])
                self.mean = sb(f"{name}_mean", [128, 1])
                self.dev = sb(f"{name}_dev", [128, 1])
                self.var = sb(f"{name}_var", [128, 2])
                self.ve = sb(f"{name}_ve", [128, 1])
                self.half = sb(f"{name}_half", [128, 1])
                self.y = sb(f"{name}_y", [128, 1])
                self.t = sb(f"{name}_t", [128, 1])
                self.shift = sb(f"{name}_shift", [128, 1])
                self.stat = sem(f"{name}_stat")
                self.mv_ready = sem(f"{name}_mv_ready")
                self.var_ready = sem(f"{name}_var_ready")
                self.ready = sem(f"{name}_ready")
                self.ready_steps = sem(f"{name}_steps")
                self.applied = sem(f"{name}_applied")

        gn1, gn2 = Norm("gn1", TILES), Norm("gn2", ROWS + 1)

        const_in = sem("const_in")
        setup_v = sem("setup_v")
        rel_zeroed = sem("rel_zeroed")
        tap_sums, channel_max, channel_max_all = sem("tap_sums"), sem("channel_max"), sem("channel_max_all")
        qkv_scaled, proj_turned, proj_scaled = sem("qkv_scaled"), sem("proj_turned"), sem("proj_scaled")
        setup_pe = sem("setup_pe")
        setup_pool = sem("setup_pool")
        setup_done = sem("setup_done")
        x_loaded = [sem(f"x_loaded{t}") for t in range(TILES)]
        x_stored = [sem(f"x_stored{t}") for t in range(TILES)]
        misc_ready, misc_free = sem("misc_ready"), sem("misc_free")
        qkv_ready, qkv_free = sem("qkv_ready"), sem("qkv_free")
        dve_held, pool_held = sem("dve_held"), sem("pool_held")
        scores_ready = sem("scores_ready")
        biased = sem("biased")
        max_ready = sem("max_ready")
        sub_ready = sem("sub_ready")
        probs_ready = sem("probs_ready")
        probsT_ready = sem("probsT_ready")
        probsT_sb = sem("probsT_sb")
        attn_ready = sem("attn_ready")
        recip_ready = sem("recip_ready")
        attn_norm = sem("attn_norm")
        oT_hi_ready = sem("oT_hi_ready")
        xa_free = sem("xa_free")
        xc_ready = sem("xc_ready")
        tok_hi_ready, tok_lo_ready = sem("tok_hi_ready"), sem("tok_lo_ready")
        pad_hi_ready, pad_lo_ready = sem("pad_hi_ready"), sem("pad_lo_ready")
        conv_ready = sem("conv_ready")
        conv_out = sem("conv_out")

        x_tiles = x.rearrange("n (t a) w c -> n t (a w) c", t=TILES).rearrange("n t (s p) c -> n t p s c", p=SP_)
        out_tiles = out.rearrange("n (t a) w c -> n t (a w) c", t=TILES).rearrange("n t (s p) c -> n t p s c", p=SP_)

        def flat(t):
            return t[:].rearrange("p a b -> p (a b)")

        wc_raw = flat(x_b)[:, 0:TAPS * C].rearrange("p (t c) -> p t c", c=C)
        wc_mask = flat(x_b)[:, TAPS * C:2 * TAPS * C].rearrange("p (t c) -> p t c", c=C)
        wc_k = flat(x_c)[:, 0:TAPS * C].rearrange("p (t c) -> p t c", c=C)
        wc_clip = flat(x_c)[:, TAPS * C:2 * TAPS * C].rearrange("p (t c) -> p t c", c=C)
        wc_sum = flat(x_n)[:, 0:C]
        wc_neg = flat(x_n)[:, C:2 * C]
        wc_absmax = flat(x_n)[:, 2 * C:3 * C]
        wc_chmax = flat(x_n)[:, 3 * C:4 * C]
        wc_inv = flat(x_n)[:, 4 * C:5 * C]
        ones = flat(x_n)[:, 5 * C:6 * C]
        rel_rev = flat(x_a)[:, 0:N * HEADS].rearrange("p (m h) -> p m h", h=HEADS)
        rel = flat(x_a)[:, N * HEADS:2 * N * HEADS].rearrange("p (h m) -> p h m", m=N)
        mask = flat(x_a)[:, 2 * N * HEADS:2 * N * HEADS + 2 * WP * N].rearrange("p (a w m) -> p a w m", a=2, m=N)

        block = ctx.enter_context(nc.Block())

        def over_images(eng, body):
            for i in range(-1, STEADY):
                body(i)
            with eng.Fori(STEADY, IMGS - 2) as i:
                body(i)
            for i in range(IMGS - 2, IMGS + 2):
                body(i)

        @block.sync
        def _(sp):
            loads = [
                (ident[:], ident_d), (group[:], group_d), (parity[:], parity_d),
                (w_in[:, 0:3, :], wqkv.rearrange("(t p) c -> p t c", p=128)), (w_in[:, 3, :], wproj),
                *((b_in[:, t:t + 1], bqkv[t * C:(t + 1) * C].rearrange("(p a) -> p a", a=1)) for t in range(3)),
                (b_in[:, 3:4], bproj.rearrange("(p a) -> p a", a=1)),
                (wc_raw, wconv.rearrange("a b i o -> i (a b) o")),
                (wc_mask, prune.rearrange("(t i) o -> i t o", i=C)),
                (mask, mask_d),
            ]
            for dst, src in loads:
                sp.dma_start(dst, src).then_inc(const_in, 16)
            for t in range(TILES):
                sp.dma_start(x_in[:, t * SUB:(t + 1) * SUB, :], x_tiles[0, t]).then_inc(x_loaded[t], 16)
            sp.wait_ge(rel_zeroed, 1)
            span = 2 * WIN - 1
            for half in range(2):
                for r1 in range(WIN):
                    src = bass.AP(tensor=table.tensor, offset=table.offset + r1 * span * HEADS,
                                  ap=[[HEADS, WIN], [span * HEADS, WIN], [1, WIN * HEADS]])
                    p0 = ODD * half + r1 * WIN
                    sp.dma_start(rel_rev[p0:p0 + WIN].rearrange("p (r c) h -> p r (c h)", c=WIN), src)\
                        .then_inc(const_in, 16)

            def body(i):
                for u in range(UNITS):
                    for kind, t in misc_at(i, u):
                        if kind == "tin" and live(i, 2):
                            sp.wait_ge(misc_ready, misc_number(i, kind, t) + 1)
                            sp.dma_start(x_in[:, t * SUB:(t + 1) * SUB, :], x_tiles[i + 2, t]).then_inc(x_loaded[t], 16)
                        if kind == "tout":
                            img = i - 2 if t == TILES - 1 else i - 1
                            sp.wait_ge(misc_free, misc_number(i, kind, t) + 1)
                            sp.dma_start(out_tiles[img, t], x_out[:, t * SUB:(t + 1) * SUB, :]).then_inc(x_stored[t], 16)

            over_images(sp, body)
            for t in range(TILES):
                sp.wait_ge(x_stored[t], 16 * IMGS)

        @block.gpsimd
        def _(pool):
            pool.wait_ge(channel_max, 1)
            nc.gpsimd.partition_all_reduce(wc_chmax, wc_absmax, 128, RMAX).then_inc(setup_pool, 1)

            def body(i):
                for u in range(UNITS):
                    if u == NORM2_AT and live(i, -1):
                        pool.wait_ge(gn2.ready, i)
                        pool.wait_ge(xc_ready, i)
                        if live(i):
                            pool.wait_ge(tok_lo_ready, (i + 1) * ROWS)
                        pool.sem_inc(pool_held, 1)
                        nc.gpsimd.tensor_scalar(x_n[:], x_c[:], gn2.y[:], gn2.shift[:], ALU.mult, ALU.add)\
                            .then_inc(gn2.applied, 1)
                    if u == NORM1_AT and live(i, 1):
                        pool.wait_ge(gn1.ready, i + 2)
                        need(pool, pad_lo_ready, i)
                        pool.sem_inc(pool_held, 1)
                        for rows, cols, y0, x0 in roll_pieces(H):
                            n, m = rows.stop - rows.start, cols.stop - cols.start
                            last = nc.gpsimd.tensor_scalar(x_n[:, rows, cols], x_a[:, y0:y0 + n, x0:x0 + m],
                                                           gn1.y[:], gn1.shift[:], ALU.mult, ALU.add)
                        last.then_inc(gn1.applied, 1)
                    if live(i):
                        pool.wait_ge(max_ready, i * UNITS + u + 1)
                        s = s_sb[0:QP, u % 4].rearrange("p w h m -> p (w h) m")
                        top = s_max[0:QP, u % 4].unsqueeze(2).to_broadcast((QP, 2 * WP, N))
                        nc.gpsimd.tensor_tensor(s, s, top, ALU.subtract).then_inc(sub_ready, 1)

            over_images(pool, body)

        @block.scalar
        def _(act):
            act.wait_ge(setup_done, 1)

            def exp_unit(i, g, slot):
                act.wait_ge(sub_ready, g + 1)
                need(act, probsT_ready, g - 1)
                nc.scalar.activation(probs[0:QP, slot % 2, :, :, 0:N], s_sb[0:QP, slot % 4], ACT.Exp)\
                    .then_inc(probs_ready, 1)

            def evacuate_probsT(i, g, slot):
                act.wait_ge(probsT_ready, g + 1)
                need(act, attn_ready, g - 1)
                nc.scalar.copy(probsT[:, slot % 2], probsT_ps[:].rearrange("p (w n) -> p w n", n=ODD)[:, :, 0:N])\
                    .then_inc(probsT_sb, 1)

            def body(i):
                for u in range(UNITS):
                    if live(i, 0 if u >= 1 else -1):
                        exp_unit(i, i * UNITS + (u - 1), u - 1)
                    if live(i, 0 if u >= LAG_T else -1):
                        evacuate_probsT(i, i * UNITS + (u - LAG_T), u - LAG_T)
                    for kind, t in misc_at(i, u):
                        number = misc_number(i, kind, t)
                        if kind == "ot":
                            act.wait_ge(misc_ready, number + 1)
                            nc.scalar.copy(oT_hi[:].rearrange("p r (w c) -> p w r c", c=WIN),
                                           misc_ps[:].rearrange("p (w n) -> p w n", n=ODD)[:, :, 0:N]
                                           .rearrange("p w (r c) -> p w r c", c=WIN)).then_inc(oT_hi_ready, 1)
                        if kind == "tin":
                            act.wait_ge(misc_ready, number + 1)
                            need(act, xa_free, i + 1)
                            need(act, gn1.applied, i + 1)
                            nc.scalar.copy(flat(x_a)[:, t * TP:(t + 1) * TP].rearrange("c (s p) -> c s p", s=SUB),
                                           misc_ps[:].rearrange("c (s p) -> c s p", s=SUB)[:, :, 0:SP_])\
                                .then_inc(misc_free, 1)
                        if kind == "tout":
                            img = i - 2 if t == TILES - 1 else i - 1
                            act.wait_ge(misc_ready, number + 1)
                            need(act, x_stored[t], 16 * img)
                            nc.scalar.copy(x_out[:, t * SUB:(t + 1) * SUB, :],
                                           misc_ps[0:SP_, :].rearrange("p (s c) -> p s c", s=SUB))\
                                .then_inc(misc_free, 1)
                    r, j = divmod(u, PAIRS)
                    if live(i, 0 if r < ROWS - 1 else 1):
                        number, slot = (i * ROWS + (r + 1)) * 4 + j, (r + 1) % 2
                        act.wait_ge(qkv_ready, number + 1)
                        tokens = qkv_ps[:, 0:RT].rearrange("p (w n) -> p w n", n=N)
                        if j == 0:
                            last = nc.scalar.activation(q[:, slot], tokens, ACT.Identity, bias=q_bias[:], scale=q_scale[:])
                        elif j == 1:
                            for e in range(2):
                                last = nc.scalar.activation(k[:, slot, :, e, :], tokens, ACT.Identity,
                                                            bias=k_bias[:, e:e + 1], scale=k_scale[:, e:e + 1])
                        else:
                            parts = ([(0, 4, 0, 0), (0, 4, 1, 1)] if j == 2 else
                                     [(0, 4, 4, 0), (0, 3, 5, 1), (3, 1, 0, 1)])
                            vals = qkv_ps[:].rearrange("p (w a e d) -> p w a e d", w=NWIN // 2, e=2, d=HD)
                            for b, n, w0, e in parts:
                                half = slice(ODD * e, ODD * e + ODD)
                                last = nc.scalar.copy(v[half, slot, w0:w0 + n, :, e * HD:(e + 1) * HD],
                                                      vals[half, b:b + n, :, e, :])
                        last.then_inc(qkv_free, 1)
                    if live(i, 1):
                        for row in SPLIT_AT.get(u, ()):
                            act.wait_ge(gn1.applied, i + 2)
                            need(act, qkv_ready, (i * ROWS + row + 1) * 4)
                            nc.scalar.copy(
                                tok_hi[:, row * NWIN:(row + 1) * NWIN, 0:N].rearrange("p w (r c) -> p w r c", c=WIN),
                                x_n[:, row * WIN:(row + 1) * WIN, :].rearrange("p r (w c) -> p w r c", c=WIN))\
                                .then_inc(tok_hi_ready, 1)
                    if u == NORM2_AT + 1 and live(i, -1):
                        act.wait_ge(gn2.applied, i)
                        need(act, conv_ready, (i - 1) * TILES)
                        nc.scalar.copy(pad_hi[:, 1:H + 1, 1:W + 1], x_n[:]).then_inc(pad_hi_ready, 1)

            over_images(act, body)

        @block.vector
        def _(dve):
            done = [0]

            def step(ins):
                done[0] += 1
                ins.then_inc(setup_v, 1)
                dve.wait_ge(setup_v, done[0])

            vec = nc.vector
            step(vec.memset(rel_rev, 0.0))
            dve.sem_inc(rel_zeroed, 1)
            for buf, value in ((tok_hi, 0.0), (tok_lo, 0.0), (pad_hi, 0.0), (pad_lo, 0.0), (v, 0.0), (probs, 0.0),
                               (scores_ps, 0.0), (attn_ps, 1.0)):
                vec.memset(buf[:], value)
            step(vec.memset(ones, 1.0))
            for e in range(2):
                step(vec.memset(v[ODD * e:ODD * e + N, :, :, :, 2 * HD + e:2 * HD + e + 1], 1.0))
            dve.wait_ge(const_in, 16 * N_CONST)

            wide = (128, TAPS, C)
            by_tap = "p t c -> p c t"
            step(vec.tensor_reduce(wc_sum, wc_raw.rearrange(by_tap), AX.X, ALU.add, apply_absolute_value=True))
            dve.sem_inc(tap_sums, 1)
            dve.wait_ge(setup_pe, 1)
            step(vec.tensor_scalar(wc_neg, misc_ps[:, 0:C], -1.0 / (TAPS * C), None, ALU.mult))
            step(vec.tensor_scalar(wc_k, wc_raw, 0.0, None, ALU.is_gt))
            step(vec.scalar_tensor_tensor(out=wc_k, in0=wc_raw, scalar=0.0, in1=wc_k, op0=ALU.is_lt, op1=ALU.subtract))
            step(vec.tensor_tensor(wc_k, wc_k, wc_neg.unsqueeze(1).to_broadcast(wide), ALU.mult))
            step(vec.tensor_scalar(wc_clip, wc_raw, -1.0, 1.0, ALU.max, ALU.min))
            step(vec.tensor_tensor(wc_k, wc_k, wc_clip, ALU.subtract))
            step(vec.tensor_tensor(wc_k, wc_k, wc_clip, ALU.add))
            step(vec.tensor_tensor(wc_k, wc_k, wc_mask, ALU.mult))
            step(vec.tensor_reduce(wc_absmax, wc_k.rearrange(by_tap), AX.X, ALU.max, apply_absolute_value=True))
            dve.sem_inc(channel_max, 1)
            dve.wait_ge(setup_pool, 1)
            step(vec.tensor_scalar(wc_chmax, wc_chmax, TINY, None, ALU.max))
            dve.sem_inc(channel_max_all, 1)
            step(vec.reciprocal(wc_inv, wc_chmax))
            step(vec.tensor_tensor(wc_k, wc_k, wc_inv.unsqueeze(1).to_broadcast(wide), ALU.mult))
            step(vec.tensor_copy(wc_hi[:], wc_k))
            step(vec.tensor_tensor(wc_lo[:], wc_k, wc_hi[:], ALU.subtract))
            dve.wait_ge(setup_pe, 2)
            step(vec.tensor_copy(wc_scale[:], misc_ps[:, 0:1]))

            step(vec.tensor_reduce(w_max[:, 0:3], w_in[:, 0:3, :], AX.X, ALU.max, apply_absolute_value=True))
            step(vec.tensor_scalar(w_max[:, 0:3], w_max[:, 0:3], TINY, None, ALU.max))
            step(vec.reciprocal(w_inv[:, 0:3], w_max[:, 0:3]))
            for t in range(3):
                step(vec.tensor_scalar(w_f[:, t, :], w_in[:, t, :], w_inv[:, t:t + 1], None, ALU.mult))
            dve.sem_inc(qkv_scaled, 1)
            dve.wait_ge(setup_pe, 3)
            step(vec.tensor_copy(w_f[:, 0:3, :], misc_ps[:, 0:3 * C].rearrange("p (t c) -> p t c", c=C)))
            step(vec.tensor_copy(w_in[:, 3, :], misc_ps[:, 3 * C:4 * C]))
            step(vec.tensor_scalar(w_f[:, 3, :], w_in[:, 3, :], w_max[:, 2:3], None, ALU.mult))
            step(vec.tensor_copy(bv2[:], b_in[:, 2:3].to_broadcast((128, 2))))
            dve.sem_inc(proj_turned, 1)
            dve.wait_ge(setup_pe, 4)
            step(vec.tensor_tensor(out_bias[:], misc_ps[:, C:C + 1], b_in[:, 3:4], ALU.add))
            step(vec.tensor_reduce(w_max[:, 3:4], misc_ps[:, 0:C], AX.X, ALU.max, apply_absolute_value=True))
            step(vec.tensor_scalar(w_max[:, 3:4], w_max[:, 3:4], TINY, None, ALU.max))
            step(vec.reciprocal(w_inv[:, 3:4], w_max[:, 3:4]))
            step(vec.tensor_scalar(w_in[:, 3, :], misc_ps[:, 0:C], w_inv[:, 3:4], None, ALU.mult))
            dve.sem_inc(proj_scaled, 1)
            dve.wait_ge(setup_pe, 5)
            step(vec.tensor_copy(w_f[:, 3, :], misc_ps[:, 0:C]))
            step(vec.tensor_copy(wT_hi[:], w_f[:]))
            step(vec.tensor_tensor(wT_lo[:], w_f[:], wT_hi[:], ALU.subtract))
            step(vec.tensor_scalar(q_scale[:], w_max[:, 0:1], HD ** -0.5, None, ALU.mult))
            step(vec.tensor_scalar(q_bias[:], b_in[:, 0:1], HD ** -0.5, None, ALU.mult))
            step(vec.tensor_scalar(k_scale[:], parity[:], w_max[:, 1:2], None, ALU.mult))
            step(vec.tensor_scalar(k_bias[:], parity[:], b_in[:, 1:2], None, ALU.mult))
            for m in range(N):
                last = vec.tensor_copy(rel[0:QP, :, m], rel_rev[0:QP, N - 1 - m, :])
            step(last)
            for a in range(2):
                for pair in range(PAIRS):
                    two = rel[0:QP, 2 * pair:2 * pair + 2, :]
                    last = vec.tensor_tensor(bias[0:QP, a, pair], two.unsqueeze(1).to_broadcast((QP, WP, 2, N)),
                                             mask[0:QP, a].unsqueeze(2).to_broadcast((QP, WP, 2, N)), ALU.add)
            step(last)
            vec.memset(bv2[:], 0.0).then_inc(setup_done, 1)


            def norm_first(gn, img):
                dve.wait_ge(gn.stat, (img + 1) * gn.stats.shape[1])
                need(dve, gn.applied, img)
                dve.sem_inc(dve_held, 1)
                vec.bn_aggr(gn.mv[:], gn.stats[:].rearrange("p a b -> p (a b)")).then_inc(gn.mv_ready, 1)

            def norm_second(gn, img, number):
                dve.wait_ge(misc_ready, number + 1)
                vec.tensor_copy(gn.mean[:], misc_ps[:, 0:1]).then_inc(misc_free, 1)
                dve.wait_ge(misc_free, number + 1)
                dve.wait_ge(gn.mv_ready, img + 1)
                vec.tensor_tensor(gn.dev[:], gn.mv[:, 0:1], gn.mean[:], ALU.subtract).then_inc(gn.var_ready, 1)
                dve.wait_ge(gn.var_ready, img * 3 + 1)
                for c in range(2):
                    vec.scalar_tensor_tensor(out=gn.var[:, c:c + 1], in0=gn.dev[:], scalar=gn.dev[:], in1=gn.mv[:, 1:2],
                                             op0=ALU.mult, op1=ALU.add).then_inc(gn.var_ready, 1)

            def norm_third(gn, img, number, steps):
                dve.wait_ge(misc_ready, number + 1)
                n = [0]

                def then(ins):
                    n[0] += 1
                    ins.then_inc(gn.ready_steps, 1)
                    dve.wait_ge(gn.ready_steps, img * steps + n[0])

                vec.tensor_scalar(gn.ve[:], misc_ps[:, 0:1], EPS, None, ALU.add).then_inc(misc_free, 1)
                dve.wait_ge(misc_free, number + 1)
                then(vec.tensor_scalar(gn.half[:], gn.ve[:], -0.5, None, ALU.mult))
                then(vec.tensor_scalar(gn.t[:].bitcast(I32), gn.ve[:].bitcast(I32), 1, None, ALU.logical_shift_right))
                then(vec.tensor_scalar(gn.y[:].bitcast(I32), gn.t[:].bitcast(I32), -1.0, float(RSQRT_SEED), ALU.mult, ALU.add))
                for _ in range(NEWTON):
                    then(vec.scalar_tensor_tensor(out=gn.t[:], in0=gn.y[:], scalar=gn.y[:], in1=gn.half[:],
                                                  op0=ALU.mult, op1=ALU.mult))
                    then(vec.scalar_tensor_tensor(out=gn.y[:], in0=gn.t[:], scalar=1.5, in1=gn.y[:],
                                                  op0=ALU.add, op1=ALU.mult))
                vec.scalar_tensor_tensor(out=gn.shift[:], in0=gn.mean[:], scalar=-1.0, in1=gn.y[:],
                                         op0=ALU.mult, op1=ALU.mult).then_inc(gn.ready, 1)

            norm_steps = 3 + 2 * NEWTON

            def body(i):
                for u in range(UNITS):
                    r, rest = divmod(u - OT_AT, PAIRS)
                    if rest == 0 and live(i, 0 if r >= 0 else -1):
                        row = i * ROWS + r
                        dve.wait_ge(attn_ready, (row + 1) * PAIRS)
                        banks = [attn_ps[0:QP, b, 0:2 * PAIRS * VW].rearrange("p (a v) -> p a v", v=VW) for b in range(2)]
                        for b in range(2):
                            last = vec.reciprocal(recip[0:QP, b], banks[b][:, :, 2 * HD:VW])
                        last.then_inc(recip_ready, 1)
                        dve.wait_ge(recip_ready, row + 1)
                        if not isinstance(row, int) or row > 0:
                            turn = i if u >= PAIRS else i - 1
                            dve.wait_ge(misc_ready, misc_number(turn, "ot", (r - 1) % ROWS) + 1)
                        for b in range(2):
                            last = vec.tensor_tensor(
                                o_sb[0:QP, 2 * b:2 * b + 2, :].rearrange("p w (a d) -> p (w a) d", d=HD)
                                .rearrange("p (a e) d -> p a e d", e=2),
                                banks[b][:, :, 0:2 * HD].rearrange("p a (e d) -> p a e d", d=HD),
                                recip[0:QP, b].unsqueeze(3).to_broadcast((QP, 2 * PAIRS, 2, HD)), ALU.mult)
                        last.then_inc(attn_norm, 1)
                    for t in range(TILES):
                        later, at = divmod(CONV_AT + CONV_STEPS * (t + 1), UNITS)
                        if u == at and live(i, -1 - later):
                            img = i - (1 + later)
                            dve.wait_ge(conv_ready, img * TILES + t + 1)
                            dve.wait_ge(xc_ready, img + 1)
                            tile = flat(x_c)[:, t * TP:(t + 1) * TP]
                            vec.scalar_tensor_tensor(out=tile, in0=conv_ps[:, 0:TP], scalar=wc_scale[:], in1=tile,
                                                     op0=ALU.mult, op1=ALU.add).then_inc(conv_out, 1)
                    if live(i):
                        g = i * UNITS + u
                        dve.wait_ge(scores_ready, g + 1)
                        need(dve, probs_ready, g - 3)
                        edge = int(u // PAIRS == ROWS - 1)
                        vec.tensor_tensor(s_sb[0:QP, u % 4].rearrange("p w h m -> p (w h m)"),
                                          scores_ps[0:QP, u % 2, 0:WP * 2 * N],
                                          bias[0:QP, edge, u % PAIRS].rearrange("p w h m -> p (w h m)"), ALU.add)\
                            .then_inc(biased, 1)
                        dve.wait_ge(biased, g + 1)
                        vec.tensor_reduce(s_max[0:QP, u % 4], s_sb[0:QP, u % 4].rearrange("p w h m -> p (w h) m"),
                                          AX.X, ALU.max).then_inc(max_ready, 1)
                    for kind, t in misc_at(i, u):
                        number = misc_number(i, kind, t)
                        if kind == "ot":
                            row = i * ROWS + (t if u >= OT_AT else t - ROWS)
                            dve.wait_ge(oT_hi_ready, row + 1)
                            vec.tensor_tensor(oT_lo[:].rearrange("p r (w c) -> p w r c", c=WIN),
                                              misc_ps[:].rearrange("p (w n) -> p w n", n=ODD)[:, :, 0:N]
                                              .rearrange("p w (r c) -> p w r c", c=WIN),
                                              oT_hi[:].rearrange("p r (w c) -> p w r c", c=WIN), ALU.subtract)\
                                .then_inc(misc_free, 1)
                        if kind == "proj":
                            dve.wait_ge(misc_ready, number + 1)
                            if t == 0:
                                dve.wait_ge(xa_free, i + 1)
                            pieces = list(roll_pieces(WIN, t * WIN))
                            proj = misc_ps[:, 0:RT].rearrange("p (r w) -> p r w", w=W)
                            for rows, cols, y0, x0 in pieces:
                                n, m = rows.stop - rows.start, cols.stop - cols.start
                                at = x_b[:, y0:y0 + n, x0:x0 + m]
                                last = vec.scalar_tensor_tensor(out=at, in0=proj[:, rows, cols], scalar=w_max[:, 3:4],
                                                                in1=at, op0=ALU.mult, op1=ALU.add)
                            last.then_inc(misc_free, 1)
                            dve.wait_ge(misc_free, number + 1)
                            spans = sorted({(y0, rows.stop - rows.start) for rows, _, y0, _ in pieces}, reverse=True)
                            for n, (y0, height) in enumerate(spans):
                                vec.bn_stats(gn2.stats[:, t + n, :], flat(x_b)[:, y0 * W:(y0 + height) * W])\
                                    .then_inc(gn2.stat, 1)
                            if t == ROWS - 1:
                                norm_first(gn2, i - 1)
                        if kind == "tin":
                            dve.wait_ge(misc_free, number + 1)
                            vec.bn_stats(gn1.stats[:, t, :], flat(x_a)[:, t * TP:(t + 1) * TP]).then_inc(gn1.stat, 1)
                            if t == TILES - 1:
                                norm_first(gn1, i + 1)
                        if kind in ("gn1", "gn2"):
                            gn, img = (gn1, i + 1) if kind == "gn1" else (gn2, i - 1)
                            if t == 0:
                                norm_second(gn, img, number)
                            else:
                                norm_third(gn, img, number, norm_steps)
                    if u == COPY_AT and live(i, -1):
                        if live(i, -2):
                            dve.wait_ge(misc_ready, misc_number(i, "tout", TILES - 1) + 1)
                        vec.tensor_copy(x_c[:], x_b[:]).then_inc(xc_ready, 1)
                    if u == COPY_AT + 1 and live(i):
                        need(dve, xc_ready, i)
                        vec.tensor_scalar(x_b[:], x_a[:], out_bias[:], None, ALU.add).then_inc(xa_free, 1)
                    if live(i, 1):
                        for row in SPLIT_AT.get(u, ()):
                            dve.wait_ge(tok_hi_ready, (i + 1) * ROWS + row + 1)
                            at = slice(row * NWIN, (row + 1) * NWIN)
                            vec.tensor_tensor(
                                tok_lo[:, at, 0:N].rearrange("p w (r c) -> p w r c", c=WIN),
                                x_n[:, row * WIN:(row + 1) * WIN, :].rearrange("p r (w c) -> p w r c", c=WIN),
                                tok_hi[:, at, 0:N].rearrange("p w (r c) -> p w r c", c=WIN), ALU.subtract)\
                                .then_inc(tok_lo_ready, 1)
                    if u == NORM2_AT + 1 and live(i, -1):
                        dve.wait_ge(pad_hi_ready, i)
                        vec.tensor_tensor(pad_lo[:, 1:H + 1, 1:W + 1], x_n[:], pad_hi[:, 1:H + 1, 1:W + 1], ALU.subtract)\
                            .then_inc(pad_lo_ready, 1)

            over_images(dve, body)

        @block.tensor
        def _(pe):
            mm = nc.tensor.matmul
            pe.wait_ge(const_in, 16 * N_CONST)
            pe.wait_ge(tap_sums, 1)
            mm(misc_ps[:, 0:C], ones, wc_sum, start=True, stop=True).then_inc(setup_pe, 1)
            pe.wait_ge(channel_max_all, 1)
            nc.tensor.transpose(misc_ps[:, 0:C], wc_chmax, ident[:]).then_inc(setup_pe, 1)
            pe.wait_ge(qkv_scaled, 1)
            for t in range(3):
                nc.tensor.transpose(misc_ps[:, t * C:(t + 1) * C], w_f[:, t, :], ident[:])
            nc.tensor.transpose(misc_ps[:, 3 * C:4 * C], w_in[:, 3, :], ident[:]).then_inc(setup_pe, 1)
            pe.wait_ge(proj_turned, 1)
            nc.tensor.transpose(misc_ps[:, 0:C], w_f[:, 3, :], ident[:])
            mm(misc_ps[:, C:C + 2], w_in[:, 3, :], bv2[:], start=True, stop=True).then_inc(setup_pe, 1)
            pe.wait_ge(proj_scaled, 1)
            nc.tensor.transpose(misc_ps[:, 0:C], w_in[:, 3, :], ident[:]).then_inc(setup_pe, 1)
            pe.wait_ge(setup_done, 1)

            def three(out_ps, pairs_of_parts):
                for n, (w, t) in enumerate(pairs_of_parts):
                    last = mm(out_ps, w, t, start=(n == 0), stop=(n == 2))
                return last

            def scores(i, u):
                g, (r, pair) = i * UNITS + u, divmod(u, PAIRS)
                if pair == 0:
                    pe.wait_ge(qkv_free, (i * ROWS + r) * 4 + 2)
                need(pe, biased, g - 1)
                at = slice(pair * 32, pair * 32 + 32)
                for w in range(NWIN):
                    p0 = ODD * (w % 2)
                    last = mm(scores_ps[p0:p0 + N, u % 2, (w // 2) * 2 * N:(w // 2 + 1) * 2 * N],
                              q[at, r % 2, w, :], k[at, r % 2, w].rearrange("p e m -> p (e m)"), start=True, stop=True)
                last.then_inc(scores_ready, 1)

            def turn_probs(i, u):
                g = i * UNITS + u
                pe.wait_ge(probs_ready, g + 1)
                need(pe, probsT_sb, g)
                for w in range(WP):
                    last = nc.tensor.transpose(probsT_ps[:, w * 128:w * 128 + QP],
                                               probs[0:QP, u % 2, w].rearrange("p e m -> p (e m)"), ident[0:QP, 0:QP])
                last.then_inc(probsT_ready, 1)

            def values(i, u):
                g, (r, pair) = i * UNITS + u, divmod(u, PAIRS)
                pe.wait_ge(probsT_sb, g + 1)
                if pair == 0:
                    pe.wait_ge(qkv_free, (i * ROWS + r) * 4 + 4)
                    need(pe, attn_norm, i * ROWS + r)
                for w in range(NWIN):
                    p0, wp = ODD * (w % 2), w // 2
                    at = (wp % 2) * PAIRS * VW + pair * VW
                    last = mm(attn_ps[p0:p0 + N, wp // 2, at:at + VW], probsT[:, u % 2, w, :], v[:, r % 2, w, pair, :],
                              start=True, stop=True)
                last.then_inc(attn_ready, 1)

            def qkv(i, u):
                r, j = divmod(u, PAIRS)
                row = (r + 1) % ROWS
                number = (i * ROWS + (r + 1)) * 4 + j
                need(pe, qkv_free, number)
                if j == 0:
                    pe.wait_ge(tok_lo_ready, i * ROWS + (r + 1) + 1)
                wins = slice(row * NWIN, (row + 1) * NWIN)
                if j < 2:
                    hi, lo = tok_hi[:, wins, 0:N], tok_lo[:, wins, 0:N]
                    last = three(qkv_ps[:, 0:RT].rearrange("p (w n) -> p w n", n=N),
                                 ((wT_hi[:, j, :], hi), (wT_hi[:, j, :], lo), (wT_lo[:, j, :], hi)))
                else:
                    runs = [(b * C, slice(0, 128), (j - 2) * 4 + b) for b in range(4)]
                    if j == 3:
                        runs[3:] = [(3 * C, slice(0, ODD), NWIN - 1), (3 * C, slice(ODD, 128), 0)]
                    for col, parts, w in runs:
                        at, width = (row * NWIN + w) * ODD, parts.stop - parts.start
                        hi, lo = (t[:].rearrange("p w n -> p (w n)")[:, at:at + width] for t in (tok_hi, tok_lo))
                        last = three(qkv_ps[parts, col:col + C],
                                     ((hi, wT_hi[:, 2, :]), (lo, wT_hi[:, 2, :]), (hi, wT_lo[:, 2, :])))
                last.then_inc(qkv_ready, 1)

            def misc(i, u, kind, t):
                number = misc_number(i, kind, t)
                need(pe, misc_free, number)
                if kind == "tin":
                    pe.wait_ge(x_loaded[t], (i + 2) * 16)
                    for s in range(SUB):
                        last = nc.tensor.transpose(misc_ps[:, s * 128:s * 128 + SP_], x_in[:, t * SUB + s, :],
                                                   ident[0:SP_, 0:SP_])
                if kind == "tout":
                    img = i - 2 if t == TILES - 1 else i - 1
                    pe.wait_ge(conv_out, img * TILES + t + 1)
                    for s in range(SUB):
                        at = t * TP + s * SP_
                        last = nc.tensor.transpose(misc_ps[0:SP_, s * C:(s + 1) * C], flat(x_c)[:, at:at + SP_], ident[:])
                if kind == "ot":
                    pe.wait_ge(attn_norm, i * ROWS + (t + 1 if u >= OT_AT else t + 1 - ROWS))
                    for w in range(WP):
                        last = nc.tensor.transpose(misc_ps[:, w * 128:w * 128 + QP], o_sb[0:QP, w, :], ident[0:QP, 0:QP])
                if kind == "proj":
                    hi, lo = (o[:].rearrange("p r w -> p (r w)") for o in (oT_hi, oT_lo))
                    last = three(misc_ps[:, 0:RT], ((wT_hi[:, 3, :], hi), (wT_hi[:, 3, :], lo), (wT_lo[:, 3, :], hi)))
                if kind in ("gn1", "gn2"):
                    gn, img = (gn1, i + 1) if kind == "gn1" else (gn2, i - 1)
                    if t == 0:
                        pe.wait_ge(gn.mv_ready, img + 1)
                    else:
                        pe.wait_ge(gn.var_ready, (img + 1) * 3)
                    last = mm(misc_ps[:, 0:2], group[:], gn.mv[:] if t == 0 else gn.var[:], start=True, stop=True)
                last.then_inc(misc_ready, 1)

            def conv(i, u):
                t, part = divmod(u - CONV_AT, CONV_STEPS)
                img = i - 1
                if part == 0:
                    need(pe, conv_out, img * TILES + t)
                if t == 0 and part == 0:
                    pe.wait_ge(pad_hi_ready, i)
                if t == 0 and part == 1:
                    pe.wait_ge(pad_lo_ready, i)
                w, p = ((wc_hi, pad_hi), (wc_hi, pad_lo), (wc_lo, pad_hi))[part]
                for tap in range(TAPS):
                    dy, dx = divmod(tap, 3)
                    y0 = t * TILE_ROWS + dy
                    last = mm(conv_ps[:, 0:TP].rearrange("p (r w) -> p r w", w=W), w[:, tap, :],
                              p[:, y0:y0 + TILE_ROWS, dx:dx + W],
                              start=(part == 0 and tap == 0), stop=(part == 2 and tap == TAPS - 1))
                if part == 2:
                    last.then_inc(conv_ready, 1)

            def body(i):
                for u in range(UNITS):
                    jobs = misc_at(i, u)
                    if live(i):
                        scores(i, u)
                    if live(i, 0 if u >= LAG_T else -1):
                        turn_probs(i if u >= LAG_T else i - 1, (u - LAG_T) % UNITS)
                    if jobs:
                        misc(i, u, *jobs[0])
                    if live(i, 0 if u >= LAG_PV else -1):
                        values(i if u >= LAG_PV else i - 1, (u - LAG_PV) % UNITS)
                    if live(i, 0 if u // PAIRS < ROWS - 1 else 1):
                        qkv(i, u)
                    if u >= CONV_AT and live(i, -1):
                        conv(i, u)
                    for job in jobs[1:]:
                        misc(i, u, *job)

            over_images(pe, body)


N_CONST = 12 + 2 * WIN


_INS = ["x", "L0_conv_qkv_weight", "L0_conv_qkv_bias", "L0_conv_proj_weight", "L0_conv_proj_bias",
        "L0_conv_rel_pos_table", "L1_conv_w", "L1_conv_pruning_mask"]


def _constants():
    import numpy as np

    c = np.arange(C)
    ident = np.eye(C, dtype=np.float32)
    group = (c[:, None] // 4 == c[None, :] // 4).astype(np.float32) / 4
    parity = np.stack([(c // HD) % 2 == e for e in range(2)], axis=1).astype(np.float32)
    side = np.zeros((H, W))
    cuts = ((0, H - WIN), (H - WIN, H - SHIFT), (H - SHIFT, H))
    for a, (y0, y1) in enumerate(cuts):
        for b, (x0, x1) in enumerate(cuts):
            side[y0:y1, x0:x1] = 3 * a + b
    mask = np.zeros((128, 2, WP, N), np.float32)
    for a, row in enumerate((0, ROWS - 1)):
        for w in range(NWIN):
            s = side[row * WIN:(row + 1) * WIN, w * WIN:(w + 1) * WIN].reshape(-1)
            p0 = ODD * (w % 2)
            mask[p0:p0 + N, a, w // 2] = np.where(s[:, None] != s[None, :], -100.0, 0.0)
    return {"ident": ident, "group": group, "parity": parity, "mask": mask}


def kernel(**inputs):
    import numpy as _np
    import concourse.bacc as _bacc
    from concourse import mybir as _mybir
    from concourse.bass_utils import run_bass_kernel_spmd as _run

    nc = _bacc.Bacc("TRN2", target_bir_lowering=False, num_devices=1)
    arrays, args = {}, []
    for name, a in [(n, inputs[n]) for n in _INS] + list(_constants().items()):
        a = _np.ascontiguousarray(a)
        arrays[f"in_{name}_dram"] = a
        args.append(nc.dram_tensor(f"in_{name}_dram", a.shape, _mybir.dt.from_np(a.dtype), kind="ExternalInput").ap())
    args.append(nc.dram_tensor("out_0_dram", (IMGS, H, W, C), F32, kind="ExternalOutput").ap())
    build_block(nc, *args)
    r = _run(nc, [arrays], core_ids=[0])
    return r.results[0]["out_0_dram"]
```

```python
from contextlib import ExitStack

import concourse.bass as bass
from concourse import mybir

ALU = mybir.AluOpType
ACT = mybir.ActivationFunctionType
AX = mybir.AxisListType
F32 = mybir.dt.float32
F16 = mybir.dt.float16
I32 = mybir.dt.int32
RMAX = bass.bass_isa.ReduceOp.max

IMGS, H, W, C = 32, 56, 56, 128
WIN, SHIFT, HEADS = 7, 3, 8
N = WIN * WIN
HD = C // HEADS
ROWS = H // WIN
NWIN = W // WIN
WP = NWIN // 2
PAIRS = HEADS // 2
UNITS = ROWS * PAIRS
ODD = 64
QP = ODD + N
RT = WIN * W
VW = 2 * HD + 2
TAPS = 9
TILE_ROWS = 8
TILES = H // TILE_ROWS
TP = TILE_ROWS * W
SUB = 4
SP_ = TP // SUB
PIX = H * W
PAD = W + 2
EPS = 1e-5
TINY = 1e-30
RSQRT_SEED = 0x5F3759DF
NEWTON = 3
WRAP = W - SHIFT

LAG_T, LAG_PV = 2, 3
MID, END = 0, 1
OT_AT, PROJ_AT = 7, 9
XC_AT = {3: (1, 3), 4: (3, 5), 5: (5, 6), 7: (0, 1), 8: (6, 7)}
XB_AT = {5: (1, 3), 6: (3, 6), 8: (0, 1), 9: (6, 7)}
G2_JOBS = ((6, END), (7, MID))
CHUNKS, CHUNK_ROWS = 4, H // 4
NORM2_AT = 9
TIN_JOBS = ((10, END), (11, MID), (12, END), (13, MID), (14, END), (16, MID), (18, END))
G1_JOBS = ((20, MID), (21, MID))
NORM1_AT = {22: (0, 1), 23: (2, 3), 24: (4, 5), 25: (6, 7)}
SPLIT_AT = 23
CONV_AT, CONV_STEPS = 12, 4
CONV_PARTS = ((0, 0, 6), (2, 2, 3), (2, 2, 3), (3, 4, 0))
STEADY = 2


def live(i, shift=0):
    return not isinstance(i, int) or 0 <= i + shift < IMGS


def need(eng, sem, value):
    if not isinstance(value, int) or value > 0:
        eng.wait_ge(sem, value)


def misc_jobs(i):
    jobs = []
    for r in range(ROWS):
        for first, kind in ((OT_AT, "ot"), (PROJ_AT, "proj")):
            turn, u = divmod(first + PAIRS * r, UNITS)
            if live(i, -turn):
                jobs.append(((u, END), kind, r))
    for k in range(TILES):
        turn, u = tile_done(k)
        if live(i, -1 - turn):
            jobs.append(((u, END), "tout", k))
    for shift, kind, places in ((-1, "gn2", G2_JOBS), (1, "tin", TIN_JOBS), (1, "gn1", G1_JOBS)):
        if live(i, shift):
            jobs.extend((place, kind, n) for n, place in enumerate(places))
    return sorted(jobs)


def tile_done(k):
    return divmod(CONV_AT + CONV_STEPS * (k + 1), UNITS)


def misc_number(i, kind, index):
    if isinstance(i, int):
        before, order = sum(len(misc_jobs(j)) for j in range(-1, i)), misc_jobs(i)
    else:
        order = misc_jobs(STEADY)
        before = i * len(order) + (sum(len(misc_jobs(j)) for j in range(-1, STEADY)) - STEADY * len(order))
    return before + [job[1:] for job in order].index((kind, index))


def misc_at(i, u, places=(MID, END)):
    return [job[1:] for job in misc_jobs(i if isinstance(i, int) else STEADY) if job[0][0] == u and job[0][1] in places]


def roll_pieces(rows, row0=0):
    cut = min(max(WRAP - row0, 0), rows)
    for a, b in ((0, cut), (cut, rows)):
        for c, d in ((0, WRAP), (WRAP, W)):
            if b > a:
                yield slice(a, b), slice(c, d), (row0 + a + SHIFT) % H, (c + SHIFT) % W


def build_block(nc, x, wqkv, bqkv, wproj, bproj, table, wconv, prune, ident_d, group_d, parity_d, mask_d, out):
    with ExitStack() as ctx:
        def sb(name, shape, dt=F32):
            return ctx.enter_context(nc.sbuf_tensor(name, shape, dt))

        def pb(name, shape):
            return ctx.enter_context(nc.psum_tensor(name, shape, F32))

        def sem(name):
            return ctx.enter_context(nc.semaphore(name))

        scores_ps = pb("scores_ps", [128, 2, 512])
        probsT_ps = pb("probsT_ps", [128, 512])
        attn_ps = pb("attn_ps", [128, 2, 512])
        conv_ps = pb("conv_ps", [128, 512])
        qkv_ps = pb("qkv_ps", [128, 512])
        misc_ps = pb("misc_ps", [128, 512])

        ident = sb("ident", [128, 128])
        group = sb("group", [128, 128])
        parity = sb("parity", [128, 2])
        w_in = sb("w_in", [128, 4, C])
        b_in = sb("b_in", [128, 4])
        wT_hi = sb("wT_hi", [128, 4, C], F16)
        wT_lo = sb("wT_lo", [128, 4, C], F16)
        w_f = sb("w_f", [128, 4, C])
        w_max = sb("w_max", [128, 4])
        w_inv = sb("w_inv", [128, 4])
        bv2 = sb("bv2", [128, 2])
        q_scale, q_bias = sb("q_scale", [128, 1]), sb("q_bias", [128, 1])
        k_scale, k_bias = sb("k_scale", [128, 2]), sb("k_bias", [128, 2])
        out_bias = sb("out_bias", [128, 1])
        bias = sb("bias", [128, 2, PAIRS, WP, 2, N])
        wc_hi = sb("wc_hi", [128, TAPS, C], F16)
        wc_lo = sb("wc_lo", [128, TAPS, C], F16)
        wc_scale = sb("wc_scale", [128, 1])

        x_in = sb("x_in", [SP_, TILES * SUB, C])
        x_a = sb("x_a", [128, H, W])
        x_b = sb("x_b", [128, H, W])
        x_c = sb("x_c", [128, H, W])
        result = sb("result", [128, TP])
        x_n = sb("x_n", [128, H, W])
        tok_hi = sb("tok_hi", [128, ROWS * NWIN, ODD], F16)
        tok_lo = sb("tok_lo", [128, ROWS * NWIN, ODD], F16)
        pad_hi = sb("pad_hi", [128, PAD, PAD], F16)
        pad_lo = sb("pad_lo", [128, PAD, PAD], F16)
        x_out = sb("x_out", [SP_, TILES * SUB, C])

        q = sb("q", [128, 2, NWIN, N])
        k = sb("k", [128, 2, NWIN, 2, N])
        v = sb("v", [128, 2, NWIN, PAIRS, VW])
        s_sb = sb("s_sb", [128, 4, WP, 2, N])
        s_max = sb("s_max", [128, 4, 2 * WP])
        probs = sb("probs", [128, 2, WP, 2, ODD])
        probsT = sb("probsT", [128, 2, NWIN, N])
        recip = sb("recip", [128, 2, 2 * PAIRS, 2])
        o_sb = sb("o_sb", [128, WP, C])
        oT_hi = sb("oT_hi", [128, WIN, W], F16)
        oT_lo = sb("oT_lo", [128, WIN, W], F16)

        class Norm:

            def __init__(self, name, chunks, uses):
                self.uses = uses
                self.stats = sb(f"{name}_stats", [128, chunks, 6])
                self.mv = sb(f"{name}_mv", [128, 2])
                self.mean = sb(f"{name}_mean", [128, 1])
                self.dev = sb(f"{name}_dev", [128, 1])
                self.var = sb(f"{name}_var", [128, 2])
                self.ve = sb(f"{name}_ve", [128, 1])
                self.half = sb(f"{name}_half", [128, 1])
                self.y = sb(f"{name}_y", [128, 1])
                self.t = sb(f"{name}_t", [128, 1])
                self.shift = sb(f"{name}_shift", [128, 1])
                self.stat = sem(f"{name}_stat")
                self.mv_ready = sem(f"{name}_mv_ready")
                self.var_ready = sem(f"{name}_var_ready")
                self.ready = sem(f"{name}_ready")
                self.ready_steps = sem(f"{name}_steps")
                self.applied = sem(f"{name}_applied")

        gn1, gn2 = Norm("gn1", TILES, ROWS), Norm("gn2", ROWS + 1, CHUNKS)

        const_in = sem("const_in")
        setup_v = sem("setup_v")
        rel_zeroed = sem("rel_zeroed")
        tap_sums, channel_max, channel_max_all = sem("tap_sums"), sem("channel_max"), sem("channel_max_all")
        qkv_scaled, proj_turned, proj_scaled = sem("qkv_scaled"), sem("proj_turned"), sem("proj_scaled")
        setup_pe = sem("setup_pe")
        setup_pool = sem("setup_pool")
        setup_done = sem("setup_done")
        x_loaded = [sem(f"x_loaded{t}") for t in range(TILES)]
        x_stored = [sem(f"x_stored{t}") for t in range(TILES)]
        misc_ready, misc_free = sem("misc_ready"), sem("misc_free")
        qkv_ready, qkv_free = sem("qkv_ready"), sem("qkv_free")
        dve_held, pool_held = sem("dve_held"), sem("pool_held")
        scores_ready = sem("scores_ready")
        biased = sem("biased")
        max_ready = sem("max_ready")
        sub_ready = sem("sub_ready")
        probs_ready = sem("probs_ready")
        probsT_ready = sem("probsT_ready")
        probsT_sb = sem("probsT_sb")
        attn_ready = sem("attn_ready")
        recip_ready = sem("recip_ready")
        attn_norm = sem("attn_norm")
        oT_hi_ready = sem("oT_hi_ready")
        xa_free = sem("xa_free")
        xc_ready = sem("xc_ready")
        tok_hi_ready, tok_lo_ready = sem("tok_hi_ready"), sem("tok_lo_ready")
        pad_hi_ready, pad_lo_ready = sem("pad_hi_ready"), sem("pad_lo_ready")
        conv_ready = sem("conv_ready")
        conv_out = sem("conv_out")

        x_tiles = x.rearrange("n (t a) w c -> n t (a w) c", t=TILES).rearrange("n t (s p) c -> n t p s c", p=SP_)
        out_tiles = out.rearrange("n (t a) w c -> n t (a w) c", t=TILES).rearrange("n t (s p) c -> n t p s c", p=SP_)

        def flat(t):
            return t[:].rearrange("p a b -> p (a b)")

        wc_raw = flat(x_b)[:, 0:TAPS * C].rearrange("p (t c) -> p t c", c=C)
        wc_mask = flat(x_b)[:, TAPS * C:2 * TAPS * C].rearrange("p (t c) -> p t c", c=C)
        wc_k = flat(x_c)[:, 0:TAPS * C].rearrange("p (t c) -> p t c", c=C)
        wc_clip = flat(x_c)[:, TAPS * C:2 * TAPS * C].rearrange("p (t c) -> p t c", c=C)
        wc_sum = flat(x_n)[:, 0:C]
        wc_neg = flat(x_n)[:, C:2 * C]
        wc_absmax = flat(x_n)[:, 2 * C:3 * C]
        wc_chmax = flat(x_n)[:, 3 * C:4 * C]
        wc_inv = flat(x_n)[:, 4 * C:5 * C]
        ones = flat(x_n)[:, 5 * C:6 * C]
        rel_rev = flat(x_a)[:, 0:N * HEADS].rearrange("p (m h) -> p m h", h=HEADS)
        rel = flat(x_a)[:, N * HEADS:2 * N * HEADS].rearrange("p (h m) -> p h m", m=N)
        mask = flat(x_a)[:, 2 * N * HEADS:2 * N * HEADS + 2 * WP * N].rearrange("p (a w m) -> p a w m", a=2, m=N)

        block = ctx.enter_context(nc.Block())

        def over_images(eng, body):
            for i in range(-1, STEADY):
                body(i)
            with eng.Fori(STEADY, IMGS - 2) as i:
                body(i)
            for i in range(IMGS - 2, IMGS + 2):
                body(i)

        @block.sync
        def _(sp):
            loads = [
                (ident[:], ident_d), (group[:], group_d), (parity[:], parity_d),
                (w_in[:, 0:3, :], wqkv.rearrange("(t p) c -> p t c", p=128)), (w_in[:, 3, :], wproj),
                *((b_in[:, t:t + 1], bqkv[t * C:(t + 1) * C].rearrange("(p a) -> p a", a=1)) for t in range(3)),
                (b_in[:, 3:4], bproj.rearrange("(p a) -> p a", a=1)),
                (wc_raw, wconv.rearrange("a b i o -> i (a b) o")),
                (wc_mask, prune.rearrange("(t i) o -> i t o", i=C)),
                (mask, mask_d),
            ]
            for dst, src in loads:
                sp.dma_start(dst, src).then_inc(const_in, 16)
            for t in range(TILES):
                sp.dma_start(x_in[:, t * SUB:(t + 1) * SUB, :], x_tiles[0, t]).then_inc(x_loaded[t], 16)
            sp.wait_ge(rel_zeroed, 1)
            span = 2 * WIN - 1
            for half in range(2):
                for r1 in range(WIN):
                    src = bass.AP(tensor=table.tensor, offset=table.offset + r1 * span * HEADS,
                                  ap=[[HEADS, WIN], [span * HEADS, WIN], [1, WIN * HEADS]])
                    p0 = ODD * half + r1 * WIN
                    sp.dma_start(rel_rev[p0:p0 + WIN].rearrange("p (r c) h -> p r (c h)", c=WIN), src)\
                        .then_inc(const_in, 16)

            def body(i):
                for u in range(UNITS):
                    for kind, t in misc_at(i, u):
                        if kind == "tin" and live(i, 2):
                            sp.wait_ge(misc_ready, misc_number(i, kind, t) + 1)
                            sp.dma_start(x_in[:, t * SUB:(t + 1) * SUB, :], x_tiles[i + 2, t]).then_inc(x_loaded[t], 16)
                        if kind == "tout":
                            img = i - 1 - tile_done(t)[0]
                            sp.wait_ge(misc_free, misc_number(i, kind, t) + 1)
                            sp.dma_start(out_tiles[img, t], x_out[:, t * SUB:(t + 1) * SUB, :]).then_inc(x_stored[t], 16)

            over_images(sp, body)
            for t in range(TILES):
                sp.wait_ge(x_stored[t], 16 * IMGS)

        @block.gpsimd
        def _(pool):
            pool.wait_ge(channel_max, 1)
            nc.gpsimd.partition_all_reduce(wc_chmax, wc_absmax, 128, RMAX).then_inc(setup_pool, 1)

            def body(i):
                for u in range(UNITS):
                    if live(i):
                        pool.wait_ge(max_ready, i * UNITS + u + 1)
                        s = s_sb[0:QP, u % 4].rearrange("p w h m -> p (w h) m")
                        top = s_max[0:QP, u % 4].unsqueeze(2).to_broadcast((QP, 2 * WP, N))
                        nc.gpsimd.tensor_tensor(s, s, top, ALU.subtract).then_inc(sub_ready, 1)
                    if u in range(NORM2_AT, NORM2_AT + CHUNKS) and live(i, -1):
                        if u == NORM2_AT:
                            pool.wait_ge(gn2.ready, i)
                            pool.wait_ge(xc_ready, i * len(XC_AT))
                            if live(i):
                                pool.wait_ge(tok_lo_ready, (i + 1) * ROWS)
                            pool.sem_inc(pool_held, 1)
                        rows = slice((u - NORM2_AT) * CHUNK_ROWS, (u - NORM2_AT + 1) * CHUNK_ROWS)
                        nc.gpsimd.tensor_scalar(x_n[:, rows, :], x_c[:, rows, :], gn2.y[:], gn2.shift[:], ALU.mult, ALU.add)\
                            .then_inc(gn2.applied, 1)
                    for row in NORM1_AT.get(u, ()):
                        if live(i, 1):
                            if row == 0:
                                pool.wait_ge(gn1.ready, i + 2)
                                need(pool, pad_lo_ready, i * CHUNKS)
                                pool.sem_inc(pool_held, 1)
                            for rows, cols, y0, x0 in roll_pieces(WIN, row * WIN):
                                n, m = rows.stop - rows.start, cols.stop - cols.start
                                rows = slice(row * WIN + rows.start, row * WIN + rows.stop)
                                last = nc.gpsimd.tensor_scalar(x_n[:, rows, cols], x_a[:, y0:y0 + n, x0:x0 + m],
                                                               gn1.y[:], gn1.shift[:], ALU.mult, ALU.add)
                            last.then_inc(gn1.applied, 1)

            over_images(pool, body)

        @block.scalar
        def _(act):
            act.wait_ge(setup_done, 1)

            def exp_unit(i, g, slot):
                act.wait_ge(sub_ready, g + 1)
                need(act, probsT_ready, g - 1)
                nc.scalar.activation(probs[0:QP, slot % 2, :, :, 0:N], s_sb[0:QP, slot % 4], ACT.Exp)\
                    .then_inc(probs_ready, 1)

            def evacuate_probsT(i, g, slot):
                act.wait_ge(probsT_ready, g + 1)
                need(act, attn_ready, g - 1)
                nc.scalar.copy(probsT[:, slot % 2], probsT_ps[:].rearrange("p (w n) -> p w n", n=ODD)[:, :, 0:N])\
                    .then_inc(probsT_sb, 1)

            def misc(i, u, place):
                for kind, t in misc_at(i, u, (place,)):
                    number = misc_number(i, kind, t)
                    if kind == "ot":
                        act.wait_ge(misc_ready, number + 1)
                        nc.scalar.copy(oT_hi[:].rearrange("p r (w c) -> p w r c", c=WIN),
                                       misc_ps[:].rearrange("p (w n) -> p w n", n=ODD)[:, :, 0:N]
                                       .rearrange("p w (r c) -> p w r c", c=WIN)).then_inc(oT_hi_ready, 1)
                    if kind == "tin":
                        act.wait_ge(misc_ready, number + 1)
                        need(act, xa_free, (i + 1) * len(XB_AT))
                        need(act, gn1.applied, (i + 1) * ROWS)
                        nc.scalar.copy(flat(x_a)[:, t * TP:(t + 1) * TP].rearrange("c (s p) -> c s p", s=SUB),
                                       misc_ps[:].rearrange("c (s p) -> c s p", s=SUB)[:, :, 0:SP_])\
                            .then_inc(misc_free, 1)
                    if kind == "tout":
                        img = i - 1 - tile_done(t)[0]
                        act.wait_ge(misc_ready, number + 1)
                        need(act, x_stored[t], 16 * img)
                        nc.scalar.copy(x_out[:, t * SUB:(t + 1) * SUB, :],
                                       misc_ps[0:SP_, :].rearrange("p (s c) -> p s c", s=SUB))\
                            .then_inc(misc_free, 1)

            def body(i):
                for u in range(UNITS):
                    if live(i, 0 if u >= 1 else -1):
                        exp_unit(i, i * UNITS + (u - 1), u - 1)
                    if live(i, 0 if u >= LAG_T else -1):
                        evacuate_probsT(i, i * UNITS + (u - LAG_T), u - LAG_T)
                    misc(i, u, MID)
                    r, j = divmod(u, PAIRS)
                    if live(i, 0 if r < ROWS - 1 else 1):
                        number, slot = (i * ROWS + (r + 1)) * 4 + j, (r + 1) % 2
                        act.wait_ge(qkv_ready, number + 1)
                        tokens = qkv_ps[:, 0:RT].rearrange("p (w n) -> p w n", n=N)
                        if j == 0:
                            last = nc.scalar.activation(q[:, slot], tokens, ACT.Identity, bias=q_bias[:], scale=q_scale[:])
                        elif j == 1:
                            for e in range(2):
                                last = nc.scalar.activation(k[:, slot, :, e, :], tokens, ACT.Identity,
                                                            bias=k_bias[:, e:e + 1], scale=k_scale[:, e:e + 1])
                        else:
                            parts = ([(0, 4, 0, 0), (0, 4, 1, 1)] if j == 2 else
                                     [(0, 4, 4, 0), (0, 3, 5, 1), (3, 1, 0, 1)])
                            vals = qkv_ps[:].rearrange("p (w a e d) -> p w a e d", w=NWIN // 2, e=2, d=HD)
                            for b, n, w0, e in parts:
                                half = slice(ODD * e, ODD * e + ODD)
                                last = nc.scalar.copy(v[half, slot, w0:w0 + n, :, e * HD:(e + 1) * HD],
                                                      vals[half, b:b + n, :, e, :])
                        last.then_inc(qkv_free, 1)
                    misc(i, u, END)
                    row = u - SPLIT_AT
                    if 0 <= row < ROWS and live(i, 1):
                        act.wait_ge(gn1.applied, (i + 1) * ROWS + row + 1)
                        need(act, qkv_ready, (i * ROWS + row + 1) * 4)
                        nc.scalar.copy(
                            tok_hi[:, row * NWIN:(row + 1) * NWIN, 0:N].rearrange("p w (r c) -> p w r c", c=WIN),
                            x_n[:, row * WIN:(row + 1) * WIN, :].rearrange("p r (w c) -> p w r c", c=WIN))\
                            .then_inc(tok_hi_ready, 1)
                    chunk = u - (NORM2_AT + 1)
                    if 0 <= chunk < CHUNKS and live(i, -1):
                        act.wait_ge(gn2.applied, (i - 1) * CHUNKS + chunk + 1)
                        need(act, conv_ready, (i - 1) * TILES)
                        y0 = chunk * CHUNK_ROWS
                        nc.scalar.copy(pad_hi[:, 1 + y0:1 + y0 + CHUNK_ROWS, 1:W + 1], x_n[:, y0:y0 + CHUNK_ROWS, :])\
                            .then_inc(pad_hi_ready, 1)

            over_images(act, body)

        @block.vector
        def _(dve):
            done = [0]

            def step(ins):
                done[0] += 1
                ins.then_inc(setup_v, 1)
                dve.wait_ge(setup_v, done[0])

            vec = nc.vector
            step(vec.memset(rel_rev, 0.0))
            dve.sem_inc(rel_zeroed, 1)
            for buf, value in ((tok_hi, 0.0), (tok_lo, 0.0), (pad_hi, 0.0), (pad_lo, 0.0), (v, 0.0), (probs, 0.0),
                               (scores_ps, 0.0), (attn_ps, 1.0)):
                vec.memset(buf[:], value)
            step(vec.memset(ones, 1.0))
            for e in range(2):
                step(vec.memset(v[ODD * e:ODD * e + N, :, :, :, 2 * HD + e:2 * HD + e + 1], 1.0))
            dve.wait_ge(const_in, 16 * N_CONST)

            wide = (128, TAPS, C)
            by_tap = "p t c -> p c t"
            step(vec.tensor_reduce(wc_sum, wc_raw.rearrange(by_tap), AX.X, ALU.add, apply_absolute_value=True))
            dve.sem_inc(tap_sums, 1)
            dve.wait_ge(setup_pe, 1)
            step(vec.tensor_scalar(wc_neg, misc_ps[:, 0:C], -1.0 / (TAPS * C), None, ALU.mult))
            step(vec.tensor_scalar(wc_k, wc_raw, 0.0, None, ALU.is_gt))
            step(vec.scalar_tensor_tensor(out=wc_k, in0=wc_raw, scalar=0.0, in1=wc_k, op0=ALU.is_lt, op1=ALU.subtract))
            step(vec.tensor_tensor(wc_k, wc_k, wc_neg.unsqueeze(1).to_broadcast(wide), ALU.mult))
            step(vec.tensor_scalar(wc_clip, wc_raw, -1.0, 1.0, ALU.max, ALU.min))
            step(vec.tensor_tensor(wc_k, wc_k, wc_clip, ALU.subtract))
            step(vec.tensor_tensor(wc_k, wc_k, wc_clip, ALU.add))
            step(vec.tensor_tensor(wc_k, wc_k, wc_mask, ALU.mult))
            step(vec.tensor_reduce(wc_absmax, wc_k.rearrange(by_tap), AX.X, ALU.max, apply_absolute_value=True))
            dve.sem_inc(channel_max, 1)
            dve.wait_ge(setup_pool, 1)
            step(vec.tensor_scalar(wc_chmax, wc_chmax, TINY, None, ALU.max))
            dve.sem_inc(channel_max_all, 1)
            step(vec.reciprocal(wc_inv, wc_chmax))
            step(vec.tensor_tensor(wc_k, wc_k, wc_inv.unsqueeze(1).to_broadcast(wide), ALU.mult))
            step(vec.tensor_copy(wc_hi[:], wc_k))
            step(vec.tensor_tensor(wc_lo[:], wc_k, wc_hi[:], ALU.subtract))
            dve.wait_ge(setup_pe, 2)
            step(vec.tensor_copy(wc_scale[:], misc_ps[:, 0:1]))

            step(vec.tensor_reduce(w_max[:, 0:3], w_in[:, 0:3, :], AX.X, ALU.max, apply_absolute_value=True))
            step(vec.tensor_scalar(w_max[:, 0:3], w_max[:, 0:3], TINY, None, ALU.max))
            step(vec.reciprocal(w_inv[:, 0:3], w_max[:, 0:3]))
            for t in range(3):
                step(vec.tensor_scalar(w_f[:, t, :], w_in[:, t, :], w_inv[:, t:t + 1], None, ALU.mult))
            dve.sem_inc(qkv_scaled, 1)
            dve.wait_ge(setup_pe, 3)
            step(vec.tensor_copy(w_f[:, 0:3, :], misc_ps[:, 0:3 * C].rearrange("p (t c) -> p t c", c=C)))
            step(vec.tensor_copy(w_in[:, 3, :], misc_ps[:, 3 * C:4 * C]))
            step(vec.tensor_scalar(w_f[:, 3, :], w_in[:, 3, :], w_max[:, 2:3], None, ALU.mult))
            step(vec.tensor_copy(bv2[:], b_in[:, 2:3].to_broadcast((128, 2))))
            dve.sem_inc(proj_turned, 1)
            dve.wait_ge(setup_pe, 4)
            step(vec.tensor_tensor(out_bias[:], misc_ps[:, C:C + 1], b_in[:, 3:4], ALU.add))
            step(vec.tensor_reduce(w_max[:, 3:4], misc_ps[:, 0:C], AX.X, ALU.max, apply_absolute_value=True))
            step(vec.tensor_scalar(w_max[:, 3:4], w_max[:, 3:4], TINY, None, ALU.max))
            step(vec.reciprocal(w_inv[:, 3:4], w_max[:, 3:4]))
            step(vec.tensor_scalar(w_in[:, 3, :], misc_ps[:, 0:C], w_inv[:, 3:4], None, ALU.mult))
            dve.sem_inc(proj_scaled, 1)
            dve.wait_ge(setup_pe, 5)
            step(vec.tensor_copy(w_f[:, 3, :], misc_ps[:, 0:C]))
            step(vec.tensor_copy(wT_hi[:], w_f[:]))
            step(vec.tensor_tensor(wT_lo[:], w_f[:], wT_hi[:], ALU.subtract))
            step(vec.tensor_scalar(q_scale[:], w_max[:, 0:1], HD ** -0.5, None, ALU.mult))
            step(vec.tensor_scalar(q_bias[:], b_in[:, 0:1], HD ** -0.5, None, ALU.mult))
            step(vec.tensor_scalar(k_scale[:], parity[:], w_max[:, 1:2], None, ALU.mult))
            step(vec.tensor_scalar(k_bias[:], parity[:], b_in[:, 1:2], None, ALU.mult))
            for m in range(N):
                last = vec.tensor_copy(rel[0:QP, :, m], rel_rev[0:QP, N - 1 - m, :])
            step(last)
            for a in range(2):
                for pair in range(PAIRS):
                    two = rel[0:QP, 2 * pair:2 * pair + 2, :]
                    last = vec.tensor_tensor(bias[0:QP, a, pair], two.unsqueeze(1).to_broadcast((QP, WP, 2, N)),
                                             mask[0:QP, a].unsqueeze(2).to_broadcast((QP, WP, 2, N)), ALU.add)
            step(last)
            vec.memset(bv2[:], 0.0).then_inc(setup_done, 1)


            def norm_first(gn, img):
                dve.wait_ge(gn.stat, (img + 1) * gn.stats.shape[1])
                need(dve, gn.applied, img * gn.uses)
                dve.sem_inc(dve_held, 1)
                vec.bn_aggr(gn.mv[:], gn.stats[:].rearrange("p a b -> p (a b)")).then_inc(gn.mv_ready, 1)

            def norm_second(gn, img, number):
                dve.wait_ge(misc_ready, number + 1)
                vec.tensor_copy(gn.mean[:], misc_ps[:, 0:1]).then_inc(misc_free, 1)
                dve.wait_ge(misc_free, number + 1)
                dve.wait_ge(gn.mv_ready, img + 1)
                vec.tensor_tensor(gn.dev[:], gn.mv[:, 0:1], gn.mean[:], ALU.subtract).then_inc(gn.var_ready, 1)
                dve.wait_ge(gn.var_ready, img * 3 + 1)
                for c in range(2):
                    vec.scalar_tensor_tensor(out=gn.var[:, c:c + 1], in0=gn.dev[:], scalar=gn.dev[:], in1=gn.mv[:, 1:2],
                                             op0=ALU.mult, op1=ALU.add).then_inc(gn.var_ready, 1)

            def norm_third(gn, img, number, steps):
                dve.wait_ge(misc_ready, number + 1)
                n = [0]

                def then(ins):
                    n[0] += 1
                    ins.then_inc(gn.ready_steps, 1)
                    dve.wait_ge(gn.ready_steps, img * steps + n[0])

                vec.tensor_scalar(gn.ve[:], misc_ps[:, 0:1], EPS, None, ALU.add).then_inc(misc_free, 1)
                dve.wait_ge(misc_free, number + 1)
                then(vec.tensor_scalar(gn.half[:], gn.ve[:], -0.5, None, ALU.mult))
                then(vec.tensor_scalar(gn.t[:].bitcast(I32), gn.ve[:].bitcast(I32), 1, None, ALU.logical_shift_right))
                then(vec.tensor_scalar(gn.y[:].bitcast(I32), gn.t[:].bitcast(I32), -1.0, float(RSQRT_SEED), ALU.mult, ALU.add))
                for _ in range(NEWTON):
                    then(vec.scalar_tensor_tensor(out=gn.t[:], in0=gn.y[:], scalar=gn.y[:], in1=gn.half[:],
                                                  op0=ALU.mult, op1=ALU.mult))
                    then(vec.scalar_tensor_tensor(out=gn.y[:], in0=gn.t[:], scalar=1.5, in1=gn.y[:],
                                                  op0=ALU.add, op1=ALU.mult))
                vec.scalar_tensor_tensor(out=gn.shift[:], in0=gn.mean[:], scalar=-1.0, in1=gn.y[:],
                                         op0=ALU.mult, op1=ALU.mult).then_inc(gn.ready, 1)

            norm_steps = 3 + 2 * NEWTON

            def body(i):
                for u in range(UNITS):
                    r, rest = divmod(u - OT_AT, PAIRS)
                    if rest == 0 and live(i, 0 if r >= 0 else -1):
                        row = i * ROWS + r
                        dve.wait_ge(attn_ready, (row + 1) * PAIRS)
                        banks = [attn_ps[0:QP, b, 0:2 * PAIRS * VW].rearrange("p (a v) -> p a v", v=VW) for b in range(2)]
                        for b in range(2):
                            last = vec.reciprocal(recip[0:QP, b], banks[b][:, :, 2 * HD:VW])
                        last.then_inc(recip_ready, 1)
                        dve.wait_ge(recip_ready, row + 1)
                        if not isinstance(row, int) or row > 0:
                            turn = i if u >= PAIRS else i - 1
                            dve.wait_ge(misc_ready, misc_number(turn, "ot", (r - 1) % ROWS) + 1)
                        for b in range(2):
                            last = vec.tensor_tensor(
                                o_sb[0:QP, 2 * b:2 * b + 2, :].rearrange("p w (a d) -> p (w a) d", d=HD)
                                .rearrange("p (a e) d -> p a e d", e=2),
                                banks[b][:, :, 0:2 * HD].rearrange("p a (e d) -> p a e d", d=HD),
                                recip[0:QP, b].unsqueeze(3).to_broadcast((QP, 2 * PAIRS, 2, HD)), ALU.mult)
                        last.then_inc(attn_norm, 1)
                    for t in range(TILES):
                        turn, at = tile_done(t)
                        if u == at and live(i, -1 - turn):
                            img = i - 1 - turn
                            dve.wait_ge(conv_ready, img * TILES + t + 1)
                            dve.wait_ge(xc_ready, (img + 1) * len(XC_AT))
                            if t > 0 or not isinstance(img, int) or img > 0:
                                before = i - turn + (tile_done(t - 1)[0] if t > 0 else tile_done(TILES - 1)[0] - 1)
                                dve.wait_ge(misc_ready, misc_number(before, "tout", (t - 1) % TILES) + 1)
                            vec.scalar_tensor_tensor(out=result[:], in0=conv_ps[:, 0:TP], scalar=wc_scale[:],
                                                     in1=flat(x_c)[:, t * TP:(t + 1) * TP], op0=ALU.mult, op1=ALU.add)\
                                .then_inc(conv_out, 1)
                    if live(i):
                        g = i * UNITS + u
                        dve.wait_ge(scores_ready, g + 1)
                        need(dve, probs_ready, g - 3)
                        edge = int(u // PAIRS == ROWS - 1)
                        vec.tensor_tensor(s_sb[0:QP, u % 4].rearrange("p w h m -> p (w h m)"),
                                          scores_ps[0:QP, u % 2, 0:WP * 2 * N],
                                          bias[0:QP, edge, u % PAIRS].rearrange("p w h m -> p (w h m)"), ALU.add)\
                            .then_inc(biased, 1)
                        dve.wait_ge(biased, g + 1)
                        vec.tensor_reduce(s_max[0:QP, u % 4], s_sb[0:QP, u % 4].rearrange("p w h m -> p (w h) m"),
                                          AX.X, ALU.max).then_inc(max_ready, 1)
                    if u in XC_AT and live(i, -1):
                        t0, t1 = XC_AT[u]
                        need(dve, conv_out, (i - 2) * TILES + t1)
                        vec.tensor_copy(flat(x_c)[:, t0 * TP:t1 * TP], flat(x_b)[:, t0 * TP:t1 * TP]).then_inc(xc_ready, 1)
                    if u in XB_AT and live(i):
                        t0, t1 = XB_AT[u]
                        copied = [tiles[1] for tiles in XC_AT.values()].index(t1) + 1
                        need(dve, xc_ready, (i - 1) * len(XC_AT) + copied)
                        need(dve, gn2.stat, i * (ROWS + 1) - (2 if 0 < t0 and t1 < TILES else 0))
                        vec.tensor_scalar(flat(x_b)[:, t0 * TP:t1 * TP], flat(x_a)[:, t0 * TP:t1 * TP],
                                          out_bias[:], None, ALU.add).then_inc(xa_free, 1)
                    row = u - (SPLIT_AT + 1)
                    if 0 <= row < ROWS and live(i, 1):
                        dve.wait_ge(tok_hi_ready, (i + 1) * ROWS + row + 1)
                        at = slice(row * NWIN, (row + 1) * NWIN)
                        vec.tensor_tensor(
                            tok_lo[:, at, 0:N].rearrange("p w (r c) -> p w r c", c=WIN),
                            x_n[:, row * WIN:(row + 1) * WIN, :].rearrange("p r (w c) -> p w r c", c=WIN),
                            tok_hi[:, at, 0:N].rearrange("p w (r c) -> p w r c", c=WIN), ALU.subtract)\
                            .then_inc(tok_lo_ready, 1)
                    chunk = u - (NORM2_AT + 2)
                    if 0 <= chunk < CHUNKS and live(i, -1):
                        dve.wait_ge(pad_hi_ready, (i - 1) * CHUNKS + chunk + 1)
                        rows = slice(chunk * CHUNK_ROWS, (chunk + 1) * CHUNK_ROWS)
                        inner = slice(1 + rows.start, 1 + rows.stop)
                        vec.tensor_tensor(pad_lo[:, inner, 1:W + 1], x_n[:, rows, :], pad_hi[:, inner, 1:W + 1],
                                          ALU.subtract).then_inc(pad_lo_ready, 1)
                    for kind, t in misc_at(i, u):
                        number = misc_number(i, kind, t)
                        if kind == "ot":
                            row = i * ROWS + (t if u >= OT_AT else t - ROWS)
                            dve.wait_ge(oT_hi_ready, row + 1)
                            vec.tensor_tensor(oT_lo[:].rearrange("p r (w c) -> p w r c", c=WIN),
                                              misc_ps[:].rearrange("p (w n) -> p w n", n=ODD)[:, :, 0:N]
                                              .rearrange("p w (r c) -> p w r c", c=WIN),
                                              oT_hi[:].rearrange("p r (w c) -> p w r c", c=WIN), ALU.subtract)\
                                .then_inc(misc_free, 1)
                        if kind == "proj":
                            dve.wait_ge(misc_ready, number + 1)
                            if t == 0:
                                dve.wait_ge(xa_free, (i + 1) * len(XB_AT))
                            pieces = list(roll_pieces(WIN, t * WIN))
                            proj = misc_ps[:, 0:RT].rearrange("p (r w) -> p r w", w=W)
                            for rows, cols, y0, x0 in pieces:
                                n, m = rows.stop - rows.start, cols.stop - cols.start
                                at = x_b[:, y0:y0 + n, x0:x0 + m]
                                last = vec.scalar_tensor_tensor(out=at, in0=proj[:, rows, cols], scalar=w_max[:, 3:4],
                                                                in1=at, op0=ALU.mult, op1=ALU.add)
                            last.then_inc(misc_free, 1)
                            dve.wait_ge(misc_free, number + 1)
                            spans = sorted({(y0, rows.stop - rows.start) for rows, _, y0, _ in pieces}, reverse=True)
                            for n, (y0, height) in enumerate(spans):
                                vec.bn_stats(gn2.stats[:, t + n, :], flat(x_b)[:, y0 * W:(y0 + height) * W])\
                                    .then_inc(gn2.stat, 1)
                            if t == ROWS - 1:
                                norm_first(gn2, i - 1)
                        if kind == "tin":
                            dve.wait_ge(misc_free, number + 1)
                            vec.bn_stats(gn1.stats[:, t, :], flat(x_a)[:, t * TP:(t + 1) * TP]).then_inc(gn1.stat, 1)
                            if t == TILES - 1:
                                norm_first(gn1, i + 1)
                        if kind in ("gn1", "gn2"):
                            gn, img = (gn1, i + 1) if kind == "gn1" else (gn2, i - 1)
                            if t == 0:
                                norm_second(gn, img, number)
                            else:
                                norm_third(gn, img, number, norm_steps)

            over_images(dve, body)

        @block.tensor
        def _(pe):
            mm = nc.tensor.matmul
            pe.wait_ge(const_in, 16 * N_CONST)
            pe.wait_ge(tap_sums, 1)
            mm(misc_ps[:, 0:C], ones, wc_sum, start=True, stop=True).then_inc(setup_pe, 1)
            pe.wait_ge(channel_max_all, 1)
            nc.tensor.transpose(misc_ps[:, 0:C], wc_chmax, ident[:]).then_inc(setup_pe, 1)
            pe.wait_ge(qkv_scaled, 1)
            for t in range(3):
                nc.tensor.transpose(misc_ps[:, t * C:(t + 1) * C], w_f[:, t, :], ident[:])
            nc.tensor.transpose(misc_ps[:, 3 * C:4 * C], w_in[:, 3, :], ident[:]).then_inc(setup_pe, 1)
            pe.wait_ge(proj_turned, 1)
            nc.tensor.transpose(misc_ps[:, 0:C], w_f[:, 3, :], ident[:])
            mm(misc_ps[:, C:C + 2], w_in[:, 3, :], bv2[:], start=True, stop=True).then_inc(setup_pe, 1)
            pe.wait_ge(proj_scaled, 1)
            nc.tensor.transpose(misc_ps[:, 0:C], w_in[:, 3, :], ident[:]).then_inc(setup_pe, 1)
            pe.wait_ge(setup_done, 1)

            def three(out_ps, pairs_of_parts):
                for n, (w, t) in enumerate(pairs_of_parts):
                    last = mm(out_ps, w, t, start=(n == 0), stop=(n == 2))
                return last

            def scores(i, u):
                g, (r, pair) = i * UNITS + u, divmod(u, PAIRS)
                if pair == 0:
                    pe.wait_ge(qkv_free, (i * ROWS + r) * 4 + 2)
                need(pe, biased, g - 1)
                at = slice(pair * 32, pair * 32 + 32)
                for w in range(NWIN):
                    p0 = ODD * (w % 2)
                    last = mm(scores_ps[p0:p0 + N, u % 2, (w // 2) * 2 * N:(w // 2 + 1) * 2 * N],
                              q[at, r % 2, w, :], k[at, r % 2, w].rearrange("p e m -> p (e m)"), start=True, stop=True)
                last.then_inc(scores_ready, 1)

            def turn_probs(i, u):
                g = i * UNITS + u
                pe.wait_ge(probs_ready, g + 1)
                need(pe, probsT_sb, g)
                for w in range(WP):
                    last = nc.tensor.transpose(probsT_ps[:, w * 128:w * 128 + QP],
                                               probs[0:QP, u % 2, w].rearrange("p e m -> p (e m)"), ident[0:QP, 0:QP])
                last.then_inc(probsT_ready, 1)

            def values(i, u):
                g, (r, pair) = i * UNITS + u, divmod(u, PAIRS)
                pe.wait_ge(probsT_sb, g + 1)
                if pair == 0:
                    pe.wait_ge(qkv_free, (i * ROWS + r) * 4 + 4)
                    need(pe, attn_norm, i * ROWS + r)
                for w in range(NWIN):
                    p0, wp = ODD * (w % 2), w // 2
                    at = (wp % 2) * PAIRS * VW + pair * VW
                    last = mm(attn_ps[p0:p0 + N, wp // 2, at:at + VW], probsT[:, u % 2, w, :], v[:, r % 2, w, pair, :],
                              start=True, stop=True)
                last.then_inc(attn_ready, 1)

            def qkv(i, u):
                r, j = divmod(u, PAIRS)
                row = (r + 1) % ROWS
                number = (i * ROWS + (r + 1)) * 4 + j
                need(pe, qkv_free, number)
                if j == 0:
                    pe.wait_ge(tok_lo_ready, i * ROWS + (r + 1) + 1)
                wins = slice(row * NWIN, (row + 1) * NWIN)
                if j < 2:
                    hi, lo = tok_hi[:, wins, 0:N], tok_lo[:, wins, 0:N]
                    last = three(qkv_ps[:, 0:RT].rearrange("p (w n) -> p w n", n=N),
                                 ((wT_hi[:, j, :], hi), (wT_hi[:, j, :], lo), (wT_lo[:, j, :], hi)))
                else:
                    runs = [(b * C, slice(0, 128), (j - 2) * 4 + b) for b in range(4)]
                    if j == 3:
                        runs[3:] = [(3 * C, slice(0, ODD), NWIN - 1), (3 * C, slice(ODD, 128), 0)]
                    for col, parts, w in runs:
                        at, width = (row * NWIN + w) * ODD, parts.stop - parts.start
                        hi, lo = (t[:].rearrange("p w n -> p (w n)")[:, at:at + width] for t in (tok_hi, tok_lo))
                        last = three(qkv_ps[parts, col:col + C],
                                     ((hi, wT_hi[:, 2, :]), (lo, wT_hi[:, 2, :]), (hi, wT_lo[:, 2, :])))
                last.then_inc(qkv_ready, 1)

            def misc(i, u, kind, t):
                number = misc_number(i, kind, t)
                need(pe, misc_free, number)
                if kind == "tin":
                    pe.wait_ge(x_loaded[t], (i + 2) * 16)
                    for s in range(SUB):
                        last = nc.tensor.transpose(misc_ps[:, s * 128:s * 128 + SP_], x_in[:, t * SUB + s, :],
                                                   ident[0:SP_, 0:SP_])
                if kind == "tout":
                    img = i - 1 - tile_done(t)[0]
                    pe.wait_ge(conv_out, img * TILES + t + 1)
                    for s in range(SUB):
                        last = nc.tensor.transpose(misc_ps[0:SP_, s * C:(s + 1) * C], result[:, s * SP_:(s + 1) * SP_], ident[:])
                if kind == "ot":
                    pe.wait_ge(attn_norm, i * ROWS + (t + 1 if u >= OT_AT else t + 1 - ROWS))
                    for w in range(WP):
                        last = nc.tensor.transpose(misc_ps[:, w * 128:w * 128 + QP], o_sb[0:QP, w, :], ident[0:QP, 0:QP])
                if kind == "proj":
                    hi, lo = (o[:].rearrange("p r w -> p (r w)") for o in (oT_hi, oT_lo))
                    last = three(misc_ps[:, 0:RT], ((wT_hi[:, 3, :], hi), (wT_hi[:, 3, :], lo), (wT_lo[:, 3, :], hi)))
                if kind in ("gn1", "gn2"):
                    gn, img = (gn1, i + 1) if kind == "gn1" else (gn2, i - 1)
                    if t == 0:
                        pe.wait_ge(gn.mv_ready, img + 1)
                    else:
                        pe.wait_ge(gn.var_ready, (img + 1) * 3)
                    last = mm(misc_ps[:, 0:2], group[:], gn.mv[:] if t == 0 else gn.var[:], start=True, stop=True)
                last.then_inc(misc_ready, 1)

            def conv(i, u, place):
                turn = 0 if u >= CONV_AT else 1
                k, at = divmod(u + turn * UNITS - CONV_AT, CONV_STEPS)
                img = i - 1 - turn
                if k >= TILES or not live(img):
                    return
                first = sum(map(sum, CONV_PARTS[:at])) + sum(CONV_PARTS[at][:place])
                chunks = img * CHUNKS + min((k + 1) * TILE_ROWS, H - 1) // CHUNK_ROWS + 1
                for n in range(first, first + CONV_PARTS[at][place]):
                    part, tap = divmod(n, TAPS)
                    if n == 0:
                        need(pe, conv_out, img * TILES + k)
                        pe.wait_ge(pad_hi_ready, chunks)
                    if n == TAPS:
                        pe.wait_ge(pad_lo_ready, chunks)
                    w, p = ((wc_hi, pad_hi), (wc_hi, pad_lo), (wc_lo, pad_hi))[part]
                    dy, dx = divmod(tap, 3)
                    y0 = k * TILE_ROWS + dy
                    last = mm(conv_ps[:, 0:TP].rearrange("p (r w) -> p r w", w=W), w[:, tap, :],
                              p[:, y0:y0 + TILE_ROWS, dx:dx + W], start=(n == 0), stop=(n == 3 * TAPS - 1))
                    if n == 3 * TAPS - 1:
                        last.then_inc(conv_ready, 1)

            def body(i):
                for u in range(UNITS):
                    if live(i):
                        scores(i, u)
                    conv(i, u, 0)
                    if live(i, 0 if u >= LAG_T else -1):
                        turn_probs(i if u >= LAG_T else i - 1, (u - LAG_T) % UNITS)
                    for job in misc_at(i, u, (MID,)):
                        misc(i, u, *job)
                    conv(i, u, 1)
                    late = (u - LAG_PV) % PAIRS == 0
                    have_values = live(i, 0 if u >= LAG_PV else -1)
                    if have_values and not late:
                        values(i if u >= LAG_PV else i - 1, (u - LAG_PV) % UNITS)
                    if live(i, 0 if u // PAIRS < ROWS - 1 else 1):
                        qkv(i, u)
                    if have_values and late:
                        values(i if u >= LAG_PV else i - 1, (u - LAG_PV) % UNITS)
                    conv(i, u, 2)
                    for job in misc_at(i, u, (END,)):
                        misc(i, u, *job)

            over_images(pe, body)


N_CONST = 12 + 2 * WIN


_INS = ["x", "L0_conv_qkv_weight", "L0_conv_qkv_bias", "L0_conv_proj_weight", "L0_conv_proj_bias",
        "L0_conv_rel_pos_table", "L1_conv_w", "L1_conv_pruning_mask"]


def _constants():
    import numpy as np

    c = np.arange(C)
    ident = np.eye(C, dtype=np.float32)
    group = (c[:, None] // 4 == c[None, :] // 4).astype(np.float32) / 4
    parity = np.stack([(c // HD) % 2 == e for e in range(2)], axis=1).astype(np.float32)
    side = np.zeros((H, W))
    cuts = ((0, H - WIN), (H - WIN, H - SHIFT), (H - SHIFT, H))
    for a, (y0, y1) in enumerate(cuts):
        for b, (x0, x1) in enumerate(cuts):
            side[y0:y1, x0:x1] = 3 * a + b
    mask = np.zeros((128, 2, WP, N), np.float32)
    for a, row in enumerate((0, ROWS - 1)):
        for w in range(NWIN):
            s = side[row * WIN:(row + 1) * WIN, w * WIN:(w + 1) * WIN].reshape(-1)
            p0 = ODD * (w % 2)
            mask[p0:p0 + N, a, w // 2] = np.where(s[:, None] != s[None, :], -100.0, 0.0)
    return {"ident": ident, "group": group, "parity": parity, "mask": mask}


def kernel(**inputs):
    import numpy as _np
    import concourse.bacc as _bacc
    from concourse import mybir as _mybir
    from concourse.bass_utils import run_bass_kernel_spmd as _run

    nc = _bacc.Bacc("TRN2", target_bir_lowering=False, num_devices=1)
    arrays, args = {}, []
    for name, a in [(n, inputs[n]) for n in _INS] + list(_constants().items()):
        a = _np.ascontiguousarray(a)
        arrays[f"in_{name}_dram"] = a
        args.append(nc.dram_tensor(f"in_{name}_dram", a.shape, _mybir.dt.from_np(a.dtype), kind="ExternalInput").ap())
    args.append(nc.dram_tensor("out_0_dram", (IMGS, H, W, C), F32, kind="ExternalOutput").ap())
    build_block(nc, *args)
    r = _run(nc, [arrays], core_ids=[0])
    return r.results[0]["out_0_dram"]
```

```python
from contextlib import ExitStack

import concourse.bass as bass
from concourse import mybir

ALU = mybir.AluOpType
ACT = mybir.ActivationFunctionType
AX = mybir.AxisListType
F32 = mybir.dt.float32
F16 = mybir.dt.float16
I32 = mybir.dt.int32
RMAX = bass.bass_isa.ReduceOp.max

IMGS, H, W, C = 32, 56, 56, 128
WIN, SHIFT, HEADS = 7, 3, 8
N = WIN * WIN
HD = C // HEADS
ROWS = H // WIN
NWIN = W // WIN
WP = NWIN // 2
PAIRS = HEADS // 2
UNITS = ROWS * PAIRS
ODD = 64
QP = ODD + N
RT = WIN * W
VW = 2 * HD + 2
TAPS = 9
PLANES, KW = 4, 3
TILE_ROWS = 8
TILES = H // TILE_ROWS
TP = TILE_ROWS * W
TPAIRS = TILE_ROWS // 2
PP = TPAIRS * W
SUB = 4
SP_ = TP // SUB
PAD = W + 2
EPS = 1e-5
TINY = 1e-30
RSQRT_SEED = 0x5F3759DF
NEWTON = 3
WRAP = W - SHIFT

LAG_T, LAG_PV = 2, 3
MID, END = 0, 1
OT_AT, PROJ_AT = 7, 9
XC_AT = {2: (1, 3), 3: (3, 5), 4: (5, 6), 6: (0, 1), 8: (6, 7)}
XB_AT = {3: (1, 3), 4: (3, 6), 6: (0, 1), 12: (6, 7)}
G2_JOBS = ((6, END), (7, MID))
NORM2_AT = 9
VHI_AT, VLO_AT = 10, 12
TIN_JOBS = ((10, END), (12, END), (14, MID), (14, END), (15, MID), (17, MID), (18, END))
G1_JOBS = ((21, MID), (22, END))
NORM1_AT, HI_AT, LO_AT = 23, 24, 26
CONV_AT, CONV_STEPS = 12, 4
TOUT_LAG = 0
PLANE_ORDER = (1, 0, 2, 3)
CONV_PARTS = ((0, 2, 4), (3, 4, 5), (2, 2, 2), (6, 6, 0))
STEADY = 2


def live(i, shift=0):
    return not isinstance(i, int) or 0 <= i + shift < IMGS


def need(eng, sem, value):
    if not isinstance(value, int) or value > 0:
        eng.wait_ge(sem, value)


def misc_jobs(i):
    jobs = []
    for r in range(ROWS):
        for first, kind in ((OT_AT, "ot"), (PROJ_AT, "proj")):
            turn, u = divmod(first + PAIRS * r, UNITS)
            if live(i, -turn):
                jobs.append(((u, END), kind, r))
    for k in range(TILES):
        turn, u = tile_turned(k)
        if live(i, -1 - turn):
            jobs.append(((u, END), "tout", k))
    for shift, kind, places in ((-1, "gn2", G2_JOBS), (1, "tin", TIN_JOBS), (1, "gn1", G1_JOBS)):
        if live(i, shift):
            jobs.extend((place, kind, n) for n, place in enumerate(places))
    return sorted(jobs)


def tile_done(k):
    return divmod(CONV_AT + CONV_STEPS * (k + 1) - 1, UNITS)


def tile_turned(k):
    return divmod(CONV_AT + CONV_STEPS * (k + 1) + TOUT_LAG, UNITS)


def half_done(k):
    return divmod(CONV_AT + CONV_STEPS * (k + 1) - 2, UNITS)


def misc_number(i, kind, index):
    if isinstance(i, int):
        before, order = sum(len(misc_jobs(j)) for j in range(-1, i)), misc_jobs(i)
    else:
        order = misc_jobs(STEADY)
        before = i * len(order) + (sum(len(misc_jobs(j)) for j in range(-1, STEADY)) - STEADY * len(order))
    return before + [job[1:] for job in order].index((kind, index))


def misc_at(i, u, places=(MID, END)):
    return [job[1:] for job in misc_jobs(i if isinstance(i, int) else STEADY) if job[0][0] == u and job[0][1] in places]


def roll_pieces(rows, row0=0):
    cut = min(max(WRAP - row0, 0), rows)
    for a, b in ((0, cut), (cut, rows)):
        for c, d in ((0, WRAP), (WRAP, W)):
            if b > a:
                yield slice(a, b), slice(c, d), (row0 + a + SHIFT) % H, (c + SHIFT) % W


def build_block(nc, x, wqkv, bqkv, wproj, bproj, table, wconv, prune, ident_d, group_d, parity_d, mask_d, out):
    with ExitStack() as ctx:
        def sb(name, shape, dt=F32):
            return ctx.enter_context(nc.sbuf_tensor(name, shape, dt))

        def pb(name, shape):
            return ctx.enter_context(nc.psum_tensor(name, shape, F32))

        def sem(name):
            return ctx.enter_context(nc.semaphore(name))

        scores_ps = pb("scores_ps", [128, 2, 512])
        probsT_ps = pb("probsT_ps", [128, 512])
        attn_ps = pb("attn_ps", [128, 512])
        conv_ps = pb("conv_ps", [128, PLANES, 256])
        qkv_ps = pb("qkv_ps", [128, 512])
        misc_ps = pb("misc_ps", [128, 512])

        ident = sb("ident", [128, 128])
        group = sb("group", [128, 128])
        parity = sb("parity", [128, 2])
        three_halves, zero = sb("three_halves", [128, 1]), sb("zero", [128, 1])
        w_in = sb("w_in", [128, 4, C])
        b_in = sb("b_in", [128, 4])
        wT_hi = sb("wT_hi", [128, 4, C], F16)
        wT_lo = sb("wT_lo", [128, 4, C], F16)
        w_f = sb("w_f", [128, 4, C])
        w_max = sb("w_max", [128, 4])
        w_inv = sb("w_inv", [128, 4])
        bv2 = sb("bv2", [128, 2])
        q_scale, q_bias = sb("q_scale", [128, 1]), sb("q_bias", [128, 1])
        k_scale, k_bias = sb("k_scale", [128, 2]), sb("k_bias", [128, 2])
        out_bias = sb("out_bias", [128, 1])
        bias = sb("bias", [128, 2, PAIRS, WP, 2, N])
        wc_hi = sb("wc_hi", [128, PLANES * KW, C], F16)
        wc_lo = sb("wc_lo", [128, PLANES * KW, C], F16)
        wc_scale = sb("wc_scale", [128, 1])

        x_in = sb("x_in", [SP_, TILES * SUB, C])
        x_a = sb("x_a", [128, H, W])
        x_b = sb("x_b", [128, H, W])
        x_c = sb("x_c", [128, H, W])
        result = sb("result", [128, TP])
        x_n = sb("x_n", [128, H + 2, W])
        tok_hi = sb("tok_hi", [128, ROWS * NWIN, ODD], F16)
        tok_lo = sb("tok_lo", [128, ROWS * NWIN, ODD], F16)
        plane = sb("plane", [128, 2, PLANES, TPAIRS, W])
        plane_hi = sb("plane_hi", [128, PLANES, H // 2, PAD], F16)
        plane_lo = sb("plane_lo", [128, PLANES, H // 2, PAD], F16)
        m_1, m_sum, m_diff = sb("m_1", [128, PP]), sb("m_sum", [128, PP]), sb("m_diff", [128, PP])
        conv_y = sb("conv_y", [128, TPAIRS, 2, W])
        x_out = sb("x_out", [SP_, TILES * SUB, C])

        q = sb("q", [128, 2, NWIN, N])
        k = sb("k", [128, 2, NWIN, 2, N])
        v = sb("v", [128, 2, NWIN, PAIRS, VW])
        s_sb = sb("s_sb", [128, 4, WP, 2, N])
        s_max = sb("s_max", [128, 4, 2 * WP])
        probs = sb("probs", [128, 2, WP, 2, ODD])
        probsT = sb("probsT", [128, 2, NWIN, N])
        recip = sb("recip", [128, 2, 2 * WP, 2])
        o_sb = sb("o_sb", [128, WP, C])
        oT_hi = sb("oT_hi", [128, WIN, W], F16)
        oT_lo = sb("oT_lo", [128, WIN, W], F16)

        class Norm:

            def __init__(self, name, chunks, uses):
                self.uses = uses
                self.stats = sb(f"{name}_stats", [128, chunks, 6])
                self.mv = sb(f"{name}_mv", [128, 2])
                self.mean = sb(f"{name}_mean", [128, 1])
                self.dev = sb(f"{name}_dev", [128, 1])
                self.var = sb(f"{name}_var", [128, 2])
                self.ve = sb(f"{name}_ve", [128, 1])
                self.half = sb(f"{name}_half", [128, 1])
                self.y = sb(f"{name}_y", [128, 1])
                self.t = sb(f"{name}_t", [128, 1])
                self.shift = sb(f"{name}_shift", [128, 1])
                self.stat = sem(f"{name}_stat")
                self.mv_ready = sem(f"{name}_mv_ready")
                self.var_ready = sem(f"{name}_var_ready")
                self.ready = sem(f"{name}_ready")
                self.ready_steps = sem(f"{name}_steps")
                self.newton = sem(f"{name}_newton")
                self.applied = sem(f"{name}_applied")

        gn1, gn2 = Norm("gn1", TILES, ROWS), Norm("gn2", ROWS + 1, TILES)

        const_in = sem("const_in")
        setup_v = sem("setup_v")
        rel_zeroed = sem("rel_zeroed")
        tap_sums, channel_max = sem("tap_sums"), sem("channel_max")
        qkv_scaled, proj_turned, proj_scaled = sem("qkv_scaled"), sem("proj_turned"), sem("proj_scaled")
        setup_pe = sem("setup_pe")
        setup_pool, zeroed = sem("setup_pool"), sem("zeroed")
        scales_ready, rel_ready = sem("scales_ready"), sem("rel_ready")
        setup_done = sem("setup_done")
        x_loaded = [sem(f"x_loaded{t}") for t in range(TILES)]
        x_stored = [sem(f"x_stored{t}") for t in range(TILES)]
        misc_ready, misc_free = sem("misc_ready"), sem("misc_free")
        qkv_ready, qkv_free = sem("qkv_ready"), sem("qkv_free")
        dve_held, pool_held = sem("dve_held"), sem("pool_held")
        scores_ready = sem("scores_ready")
        biased = sem("biased")
        max_ready = sem("max_ready")
        sub_ready = sem("sub_ready")
        probs_ready = sem("probs_ready")
        probsT_ready = sem("probsT_ready")
        probsT_sb = sem("probsT_sb")
        attn_ready = sem("attn_ready")
        recip_ready = sem("recip_ready")
        attn_norm = sem("attn_norm")
        oT_hi_ready = sem("oT_hi_ready")
        xa_free = sem("xa_free")
        xc_ready = sem("xc_ready")
        tok_hi_ready, tok_lo_ready = sem("tok_hi_ready"), sem("tok_lo_ready")
        plane_ready = sem("plane_ready")
        plane_hi_ready, plane_lo_ready = sem("plane_hi_ready"), sem("plane_lo_ready")
        conv_half = sem("conv_half")
        conv_ready = sem("conv_ready")
        m1_ready = sem("m1_ready")
        conv_sums = sem("conv_sums")
        conv_out = sem("conv_out")

        x_tiles = x.rearrange("n (t a) w c -> n t (a w) c", t=TILES).rearrange("n t (s p) c -> n t p s c", p=SP_)
        out_tiles = out.rearrange("n (t a) w c -> n t (a w) c", t=TILES).rearrange("n t (s p) c -> n t p s c", p=SP_)

        def flat(t):
            return t[:].rearrange("p a b -> p (a b)")

        wc_raw = flat(x_b)[:, 0:TAPS * C].rearrange("p (t c) -> p t c", c=C)
        wc_mask = flat(x_b)[:, TAPS * C:2 * TAPS * C].rearrange("p (t c) -> p t c", c=C)
        wc_k = flat(x_c)[:, 0:TAPS * C].rearrange("p (t c) -> p t c", c=C)
        wc_clip = flat(x_c)[:, TAPS * C:2 * TAPS * C].rearrange("p (t c) -> p t c", c=C)
        wc_u = flat(x_b)[:, 0:PLANES * KW * C].rearrange("p (t c) -> p t c", c=C)
        wc_sum = flat(x_n)[:, 0:C]
        wc_neg = flat(x_n)[:, C:2 * C]
        wc_absmax = flat(x_n)[:, 2 * C:3 * C]
        wc_chmax = flat(x_c)[:, 2 * TAPS * C:(2 * TAPS + 1) * C]
        wc_inv = flat(x_n)[:, 4 * C:5 * C]
        ones = flat(x_n)[:, 5 * C:6 * C]
        rel_rev, rel, mask = (flat(x_n)[:, 6 * C + j * N * HEADS:6 * C + (j + 1) * N * HEADS] for j in range(3))
        rel_rev = rel_rev.rearrange("p (m h) -> p m h", h=HEADS)
        rel = rel.rearrange("p (h m) -> p h m", m=N)
        mask = mask.rearrange("p (a w m) -> p a w m", a=2, m=N)

        block = ctx.enter_context(nc.Block())

        def over_images(eng, body, after_first=lambda: None):
            for i in range(-1, STEADY):
                body(i)
                if i == -1:
                    after_first()
            with eng.Fori(STEADY, IMGS - 2) as i:
                body(i)
            for i in range(IMGS - 2, IMGS + 2):
                body(i)

        @block.sync
        def _(sp):
            loads = [
                (ident[:], ident_d), (group[:], group_d), (parity[:], parity_d),
                (w_in[:, 0:3, :], wqkv.rearrange("(t p) c -> p t c", p=128)), (w_in[:, 3, :], wproj),
                *((b_in[:, t:t + 1], bqkv[t * C:(t + 1) * C].rearrange("(p a) -> p a", a=1)) for t in range(3)),
                (b_in[:, 3:4], bproj.rearrange("(p a) -> p a", a=1)),
                (wc_raw, wconv.rearrange("a b i o -> i (a b) o")),
                (wc_mask, prune.rearrange("(t i) o -> i t o", i=C)),
                (mask, mask_d),
            ]
            for dst, src in loads:
                sp.dma_start(dst, src).then_inc(const_in, 16)
            for t in range(TILES):
                sp.dma_start(x_in[:, t * SUB:(t + 1) * SUB, :], x_tiles[0, t]).then_inc(x_loaded[t], 16)
            sp.wait_ge(rel_zeroed, 1)
            span = 2 * WIN - 1
            for half in range(2):
                for r1 in range(WIN):
                    src = bass.AP(tensor=table.tensor, offset=table.offset + r1 * span * HEADS,
                                  ap=[[HEADS, WIN], [span * HEADS, WIN], [1, WIN * HEADS]])
                    p0 = ODD * half + r1 * WIN
                    sp.dma_start(rel_rev[p0:p0 + WIN].rearrange("p (r c) h -> p r (c h)", c=WIN), src)\
                        .then_inc(const_in, 16)

            def body(i):
                for u in range(UNITS):
                    for kind, t in misc_at(i, u):
                        if kind == "tin" and live(i, 2):
                            sp.wait_ge(misc_ready, misc_number(i, kind, t) + 1)
                            sp.dma_start(x_in[:, t * SUB:(t + 1) * SUB, :], x_tiles[i + 2, t]).then_inc(x_loaded[t], 16)
                        if kind == "tout":
                            img = i - 1 - tile_turned(t)[0]
                            sp.wait_ge(misc_free, misc_number(i, kind, t) + 1)
                            sp.dma_start(out_tiles[img, t], x_out[:, t * SUB:(t + 1) * SUB, :]).then_inc(x_stored[t], 16)

            over_images(sp, body)
            for t in range(TILES):
                sp.wait_ge(x_stored[t], 16 * IMGS)

        @block.gpsimd
        def _(pool):
            for buf in (tok_hi, tok_lo, plane_hi, plane_lo):
                last = nc.gpsimd.memset(buf[:], 0.0)
            last.then_inc(zeroed, 1)
            pool.wait_ge(const_in, 16 * N_CONST)
            for m in range(N):
                last = nc.gpsimd.tensor_copy(rel[0:QP, :, m], rel_rev[0:QP, N - 1 - m, :])
            last.then_inc(rel_ready, 1)
            pool.wait_ge(channel_max, 1)
            nc.gpsimd.partition_all_reduce(wc_chmax, wc_absmax, 128, RMAX).then_inc(setup_pool, 1)

            def newton(gn, img):
                tt = nc.gpsimd.tensor_tensor
                done = [0]

                def then(ins):
                    done[0] += 1
                    ins.then_inc(gn.newton, 1)
                    pool.wait_ge(gn.newton, img * (4 * NEWTON + 1) + done[0])

                pool.wait_ge(gn.ready_steps, (img + 1) * 3)
                for _ in range(NEWTON):
                    then(tt(gn.t[:], gn.y[:], gn.y[:], ALU.mult))
                    then(tt(gn.t[:], gn.t[:], gn.half[:], ALU.mult))
                    then(tt(gn.t[:], gn.t[:], three_halves[:], ALU.add))
                    then(tt(gn.y[:], gn.t[:], gn.y[:], ALU.mult))
                then(tt(gn.shift[:], gn.mean[:], gn.y[:], ALU.mult))
                tt(gn.shift[:], zero[:], gn.shift[:], ALU.subtract).then_inc(gn.ready, 1)

            pool.wait_ge(setup_done, 1)

            def body(i):
                for u in range(UNITS):
                    if live(i):
                        pool.wait_ge(max_ready, i * UNITS + u + 1)
                        s = s_sb[0:QP, u % 4].rearrange("p w h m -> p (w h) m")
                        top = s_max[0:QP, u % 4].unsqueeze(2).to_broadcast((QP, 2 * WP, N))
                        nc.gpsimd.tensor_tensor(s, s, top, ALU.subtract).then_inc(sub_ready, 1)
                    for gn, jobs, shift in ((gn1, G1_JOBS, 1), (gn2, G2_JOBS, -1)):
                        if u == jobs[1][0] + 1 and live(i, shift):
                            newton(gn, i + shift)
                    t, half = divmod(u - NORM2_AT, 2)
                    if 0 <= t < TILES and live(i, -1):
                        number = (i - 1) * TILES + t
                        if half == 0:
                            if t == 0:
                                pool.wait_ge(gn2.ready, i)
                                pool.wait_ge(xc_ready, i * len(XC_AT))
                                need(pool, plane_ready, (i - 1) * TILES * 2)
                                if live(i):
                                    pool.wait_ge(tok_lo_ready, (i + 1) * ROWS)
                                pool.sem_inc(pool_held, 1)
                            y0, y1 = t * TILE_ROWS + (t > 0), min((t + 1) * TILE_ROWS + 1, H)
                            nc.gpsimd.tensor_scalar(x_n[:, 1 + y0:1 + y1, :], x_c[:, y0:y1, :], gn2.y[:], gn2.shift[:],
                                                    ALU.mult, ALU.add).then_inc(gn2.applied, 1)
                            pool.wait_ge(gn2.applied, number + 1)
                            need(pool, plane_lo_ready, ((i - 1) * TILES + max(t - 1, 0)) * 2)
                        rows = x_n[:].rearrange("p (r a) w -> p r a w", a=2)
                        d = [rows[:, t * TPAIRS + j // 2:(t + 1) * TPAIRS + j // 2, j % 2, :] for j in range(4)]
                        sums = ((d[0], d[2], ALU.subtract), (d[1], d[2], ALU.add),
                                (d[2], d[1], ALU.subtract), (d[1], d[3], ALU.subtract))
                        for j in (2 * half, 2 * half + 1):
                            last = nc.gpsimd.tensor_tensor(plane[:, t % 2, j], *sums[j])
                        last.then_inc(plane_ready, 1)
                    row = u - NORM1_AT
                    if 0 <= row < ROWS and live(i, 1):
                        if row == 0:
                            pool.wait_ge(gn1.ready, i + 2)
                            need(pool, plane_ready, i * TILES * 2)
                            pool.sem_inc(pool_held, 1)
                        for rows, cols, y0, x0 in roll_pieces(WIN, row * WIN):
                            n, m = rows.stop - rows.start, cols.stop - cols.start
                            rows = slice(1 + row * WIN + rows.start, 1 + row * WIN + rows.stop)
                            last = nc.gpsimd.tensor_scalar(x_n[:, rows, cols], x_a[:, y0:y0 + n, x0:x0 + m],
                                                           gn1.y[:], gn1.shift[:], ALU.mult, ALU.add)
                        last.then_inc(gn1.applied, 1)

            over_images(pool, body)

        @block.scalar
        def _(act):
            act.wait_ge(scales_ready, 1)
            act.wait_ge(zeroed, 1)

            def exp_unit(i, g, slot):
                act.wait_ge(sub_ready, g + 1)
                need(act, probsT_ready, g - 1)
                nc.scalar.activation(probs[0:QP, slot % 2, :, :, 0:N], s_sb[0:QP, slot % 4], ACT.Exp)\
                    .then_inc(probs_ready, 1)

            def evacuate_probsT(i, g, slot):
                act.wait_ge(probsT_ready, g + 1)
                need(act, attn_ready, g - 1)
                nc.scalar.copy(probsT[:, slot % 2], probsT_ps[:].rearrange("p (w n) -> p w n", n=ODD)[:, :, 0:N])\
                    .then_inc(probsT_sb, 1)

            def misc(i, u, place):
                for kind, t in misc_at(i, u, (place,)):
                    number = misc_number(i, kind, t)
                    if kind == "ot":
                        act.wait_ge(misc_ready, number + 1)
                        nc.scalar.copy(oT_hi[:].rearrange("p r (w c) -> p w r c", c=WIN),
                                       misc_ps[:].rearrange("p (w n) -> p w n", n=ODD)[:, :, 0:N]
                                       .rearrange("p w (r c) -> p w r c", c=WIN)).then_inc(oT_hi_ready, 1)
                    if kind == "tin":
                        act.wait_ge(misc_ready, number + 1)
                        need(act, xa_free, (i + 1) * len(XB_AT) - (t < TILES - 1))
                        need(act, gn1.applied, (i + 1) * ROWS)
                        nc.scalar.copy(flat(x_a)[:, t * TP:(t + 1) * TP].rearrange("c (s p) -> c s p", s=SUB),
                                       misc_ps[:].rearrange("c (s p) -> c s p", s=SUB)[:, :, 0:SP_])\
                            .then_inc(misc_free, 1)
                    if kind == "tout":
                        img = i - 1 - tile_turned(t)[0]
                        act.wait_ge(misc_ready, number + 1)
                        need(act, x_stored[t], 16 * img)
                        nc.scalar.copy(x_out[:, t * SUB:(t + 1) * SUB, :],
                                       misc_ps[0:SP_, :].rearrange("p (s c) -> p s c", s=SUB))\
                            .then_inc(misc_free, 1)

            def body(i):
                for u in range(UNITS):
                    if live(i, 0 if u >= 1 else -1):
                        exp_unit(i, i * UNITS + (u - 1), u - 1)
                    for t in range(TILES):
                        turn, at = half_done(t)
                        if u == at and live(i, -1 - turn):
                            number = (i - 1 - turn) * TILES + t
                            act.wait_ge(conv_half, number + 1)
                            need(act, conv_sums, number * 4)
                            nc.scalar.copy(m_1[:], conv_ps[:, 1, 0:PP]).then_inc(m1_ready, 1)
                    if live(i, 0 if u >= LAG_T else -1):
                        evacuate_probsT(i, i * UNITS + (u - LAG_T), u - LAG_T)
                    misc(i, u, MID)
                    r, j = divmod(u, PAIRS)
                    if live(i, 0 if r < ROWS - 1 else 1):
                        number, slot = (i * ROWS + (r + 1)) * 4 + j, (r + 1) % 2
                        act.wait_ge(qkv_ready, number + 1)
                        tokens = qkv_ps[:, 0:RT].rearrange("p (w n) -> p w n", n=N)
                        if j == 0:
                            last = nc.scalar.activation(q[:, slot], tokens, ACT.Identity, bias=q_bias[:], scale=q_scale[:])
                        elif j == 1:
                            for e in range(2):
                                last = nc.scalar.activation(k[:, slot, :, e, :], tokens, ACT.Identity,
                                                            bias=k_bias[:, e:e + 1], scale=k_scale[:, e:e + 1])
                        else:
                            parts = ([(0, 4, 0, 0), (0, 4, 1, 1)] if j == 2 else
                                     [(0, 4, 4, 0), (0, 3, 5, 1), (3, 1, 0, 1)])
                            vals = qkv_ps[:].rearrange("p (w a e d) -> p w a e d", w=NWIN // 2, e=2, d=HD)
                            for b, n, w0, e in parts:
                                half = slice(ODD * e, ODD * e + ODD)
                                last = nc.scalar.copy(v[half, slot, w0:w0 + n, :, e * HD:(e + 1) * HD],
                                                      vals[half, b:b + n, :, e, :])
                        last.then_inc(qkv_free, 1)
                    misc(i, u, END)
                    row = u - HI_AT
                    if 0 <= row < ROWS and live(i, 1):
                        act.wait_ge(gn1.applied, (i + 1) * ROWS + row + 1)
                        need(act, qkv_ready, (i * ROWS + row + 1) * 4)
                        nc.scalar.copy(
                            tok_hi[:, row * NWIN:(row + 1) * NWIN, 0:N].rearrange("p w (r c) -> p w r c", c=WIN),
                            x_n[:, 1 + row * WIN:1 + (row + 1) * WIN, :].rearrange("p r (w c) -> p w r c", c=WIN))\
                            .then_inc(tok_hi_ready, 1)
                    t, half = divmod(u - VHI_AT, 2)
                    if 0 <= t < TILES and live(i, -1):
                        act.wait_ge(plane_ready, ((i - 1) * TILES + t) * 2 + half + 1)
                        need(act, conv_ready, (i - 2) * TILES + t + 1)
                        two = slice(2 * half, 2 * half + 2)
                        nc.scalar.copy(plane_hi[:, two, t * TPAIRS:(t + 1) * TPAIRS, 1:W + 1], plane[:, t % 2, two])\
                            .then_inc(plane_hi_ready, 1)
                    if u in XB_AT and live(i):
                        t0, t1 = XB_AT[u]
                        copied = [tiles[1] for tiles in XC_AT.values()].index(t1) + 1
                        need(act, xc_ready, (i - 1) * len(XC_AT) + copied)
                        need(act, gn2.stat, i * (ROWS + 1) - (2 if 0 < t0 and t1 < TILES else 0))
                        nc.scalar.activation(flat(x_b)[:, t0 * TP:t1 * TP], flat(x_a)[:, t0 * TP:t1 * TP],
                                             ACT.Identity, bias=out_bias[:]).then_inc(xa_free, 1)

            over_images(act, body)

        @block.vector
        def _(dve):
            done = [0]

            def step(ins):
                done[0] += 1
                ins.then_inc(setup_v, 1)
                dve.wait_ge(setup_v, done[0])

            vec = nc.vector
            step(vec.memset(rel_rev, 0.0))
            dve.sem_inc(rel_zeroed, 1)
            for buf, value in ((v, 0.0), (probs, 0.0), (scores_ps, 0.0), (attn_ps, 1.0)):
                vec.memset(buf[:], value)
            vec.memset(three_halves[:], 1.5)
            vec.memset(zero[:], 0.0)
            step(vec.memset(ones, 1.0))
            for e in range(2):
                step(vec.memset(v[ODD * e:ODD * e + N, :, :, :, 2 * HD + e:2 * HD + e + 1], 1.0))
            dve.wait_ge(const_in, 16 * N_CONST)

            wide = (128, TAPS, C)
            by_tap = "p t c -> p c t"
            step(vec.tensor_reduce(wc_sum, wc_raw.rearrange(by_tap), AX.X, ALU.add, apply_absolute_value=True))
            dve.sem_inc(tap_sums, 1)
            dve.wait_ge(setup_pe, 1)
            step(vec.tensor_scalar(wc_neg, misc_ps[:, 0:C], -1.0 / (TAPS * C), None, ALU.mult))

            step(vec.tensor_reduce(w_max[:, 0:3], w_in[:, 0:3, :], AX.X, ALU.max, apply_absolute_value=True))
            step(vec.tensor_scalar(w_max[:, 0:3], w_max[:, 0:3], TINY, None, ALU.max))
            step(vec.reciprocal(w_inv[:, 0:3], w_max[:, 0:3]))
            for t in range(3):
                step(vec.tensor_scalar(w_f[:, t, :], w_in[:, t, :], w_inv[:, t:t + 1], None, ALU.mult))
            dve.sem_inc(qkv_scaled, 1)
            dve.wait_ge(setup_pe, 2)
            step(vec.tensor_copy(w_f[:, 0:3, :], misc_ps[:, 0:3 * C].rearrange("p (t c) -> p t c", c=C)))
            step(vec.tensor_copy(w_in[:, 3, :], misc_ps[:, 3 * C:4 * C]))
            step(vec.tensor_scalar(w_f[:, 3, :], w_in[:, 3, :], w_max[:, 2:3], None, ALU.mult))
            step(vec.tensor_copy(bv2[:], b_in[:, 2:3].to_broadcast((128, 2))))
            dve.sem_inc(proj_turned, 1)
            dve.wait_ge(setup_pe, 3)
            step(vec.tensor_tensor(out_bias[:], misc_ps[:, C:C + 1], b_in[:, 3:4], ALU.add))
            step(vec.tensor_reduce(w_max[:, 3:4], misc_ps[:, 0:C], AX.X, ALU.max, apply_absolute_value=True))
            step(vec.tensor_scalar(w_max[:, 3:4], w_max[:, 3:4], TINY, None, ALU.max))
            step(vec.reciprocal(w_inv[:, 3:4], w_max[:, 3:4]))
            step(vec.tensor_scalar(w_in[:, 3, :], misc_ps[:, 0:C], w_inv[:, 3:4], None, ALU.mult))
            dve.sem_inc(proj_scaled, 1)
            dve.wait_ge(setup_pe, 4)
            step(vec.tensor_copy(w_f[:, 3, :], misc_ps[:, 0:C]))
            step(vec.tensor_copy(wT_hi[:], w_f[:]))
            step(vec.tensor_tensor(wT_lo[:], w_f[:], wT_hi[:], ALU.subtract))
            step(vec.tensor_scalar(q_scale[:], w_max[:, 0:1], HD ** -0.5, None, ALU.mult))
            step(vec.tensor_scalar(q_bias[:], b_in[:, 0:1], HD ** -0.5, None, ALU.mult))
            step(vec.tensor_scalar(k_scale[:], parity[:], w_max[:, 1:2], None, ALU.mult))
            step(vec.tensor_scalar(k_bias[:], parity[:], b_in[:, 1:2], None, ALU.mult))
            dve.sem_inc(scales_ready, 1)

            step(vec.tensor_scalar(wc_k, wc_raw, 0.0, None, ALU.is_gt))
            step(vec.scalar_tensor_tensor(out=wc_k, in0=wc_raw, scalar=0.0, in1=wc_k, op0=ALU.is_lt, op1=ALU.subtract))
            step(vec.tensor_tensor(wc_k, wc_k, wc_neg.unsqueeze(1).to_broadcast(wide), ALU.mult))
            step(vec.tensor_scalar(wc_clip, wc_raw, -1.0, 1.0, ALU.max, ALU.min))
            step(vec.tensor_tensor(wc_k, wc_k, wc_clip, ALU.subtract))
            step(vec.tensor_tensor(wc_k, wc_k, wc_clip, ALU.add))
            step(vec.tensor_tensor(wc_k, wc_k, wc_mask, ALU.mult))
            step(vec.tensor_reduce(wc_absmax, wc_k.rearrange(by_tap), AX.X, ALU.max, apply_absolute_value=True))
            dve.sem_inc(channel_max, 1)
            dve.wait_ge(setup_pool, 1)
            step(vec.tensor_scalar(wc_chmax, wc_chmax, TINY, None, ALU.max))
            step(vec.reciprocal(wc_inv, wc_chmax))
            step(vec.tensor_tensor(wc_k, wc_k, wc_inv.unsqueeze(1).to_broadcast(wide), ALU.mult))
            g0, g1, g2 = (wc_k[:, KW * j:KW * (j + 1), :] for j in range(3))
            u0, u1, u2, u3 = (wc_u[:, KW * j:KW * (j + 1), :] for j in range(PLANES))
            step(vec.tensor_tensor(u0, g0, g2, ALU.add))
            step(vec.tensor_tensor(u1, u0, g1, ALU.add))
            step(vec.tensor_tensor(u2, u0, g1, ALU.subtract))
            step(vec.tensor_scalar(wc_u[:, KW:3 * KW, :], wc_u[:, KW:3 * KW, :], 0.5, None, ALU.mult))
            step(vec.tensor_copy(u0, g0))
            step(vec.tensor_copy(u3, g2))
            step(vec.tensor_copy(wc_hi[:], wc_u))
            step(vec.tensor_tensor(wc_lo[:], wc_u, wc_hi[:], ALU.subtract))

            dve.wait_ge(rel_ready, 1)
            for a in range(2):
                for pair in range(PAIRS):
                    two = rel[0:QP, 2 * pair:2 * pair + 2, :]
                    last = vec.tensor_tensor(bias[0:QP, a, pair], two.unsqueeze(1).to_broadcast((QP, WP, 2, N)),
                                             mask[0:QP, a].unsqueeze(2).to_broadcast((QP, WP, 2, N)), ALU.add)
            step(last)
            dve.wait_ge(zeroed, 1)
            for row in (0, H + 1):
                last = vec.memset(x_n[:, row, :], 0.0)
            last.then_inc(setup_done, 1)


            def norm_first(gn, img):
                dve.wait_ge(gn.stat, (img + 1) * gn.stats.shape[1])
                need(dve, gn.applied, img * gn.uses)
                dve.sem_inc(dve_held, 1)
                vec.bn_aggr(gn.mv[:], gn.stats[:].rearrange("p a b -> p (a b)")).then_inc(gn.mv_ready, 1)

            def norm_second(gn, img, number):
                dve.wait_ge(misc_ready, number + 1)
                vec.tensor_copy(gn.mean[:], misc_ps[:, 0:1]).then_inc(misc_free, 1)
                dve.wait_ge(misc_free, number + 1)
                dve.wait_ge(gn.mv_ready, img + 1)
                vec.tensor_tensor(gn.dev[:], gn.mv[:, 0:1], gn.mean[:], ALU.subtract).then_inc(gn.var_ready, 1)
                dve.wait_ge(gn.var_ready, img * 3 + 1)
                for c in range(2):
                    vec.scalar_tensor_tensor(out=gn.var[:, c:c + 1], in0=gn.dev[:], scalar=gn.dev[:], in1=gn.mv[:, 1:2],
                                             op0=ALU.mult, op1=ALU.add).then_inc(gn.var_ready, 1)

            def norm_third(gn, img, number, steps):
                dve.wait_ge(misc_ready, number + 1)
                n = [0]

                def then(ins):
                    n[0] += 1
                    ins.then_inc(gn.ready_steps, 1)
                    dve.wait_ge(gn.ready_steps, img * steps + n[0])

                vec.tensor_scalar(gn.ve[:], misc_ps[:, 0:1], EPS, None, ALU.add).then_inc(misc_free, 1)
                dve.wait_ge(misc_free, number + 1)
                then(vec.tensor_scalar(gn.half[:], gn.ve[:], -0.5, None, ALU.mult))
                then(vec.tensor_scalar(gn.t[:].bitcast(I32), gn.ve[:].bitcast(I32), 1, None, ALU.logical_shift_right))
                then(vec.tensor_scalar(gn.y[:].bitcast(I32), gn.t[:].bitcast(I32), -1.0, float(RSQRT_SEED), ALU.mult, ALU.add))

            norm_steps = 3

            def body(i):
                for u in range(UNITS):
                    n, rest = divmod(u - (LAG_PV + 2), 2)
                    if rest == 0 and live(i, 0 if n >= 0 else -1):
                        number, half = i * ROWS * 2 + n, n % 2
                        dve.wait_ge(attn_ready, (number + 1) * 2)
                        outputs = attn_ps[0:QP, 0:WP * 2 * VW].rearrange("p (a v) -> p a v", v=VW)
                        vec.reciprocal(recip[0:QP, half], outputs[:, :, 2 * HD:VW]).then_inc(recip_ready, 1)
                        dve.wait_ge(recip_ready, number + 1)
                        if half == 0 and (not isinstance(number, int) or number > 0):
                            turn = i if u >= 2 else i - 1
                            dve.wait_ge(misc_ready, misc_number(turn, "ot", (n // 2 - 1) % ROWS) + 1)
                        for pair in range(2):
                            at = (half * 2 + pair) * 2 * HD
                            last = vec.tensor_tensor(
                                o_sb[0:QP, :, at:at + 2 * HD].rearrange("p w (e d) -> p w e d", d=HD),
                                outputs.rearrange("p (w a) v -> p w a v", a=2)[:, :, pair, 0:2 * HD]
                                .rearrange("p w (e d) -> p w e d", d=HD),
                                recip[0:QP, half].rearrange("p (w a) e -> p w a e", a=2)[:, :, pair].unsqueeze(3)
                                .to_broadcast((QP, WP, 2, HD)), ALU.mult)
                        last.then_inc(attn_norm, 1)
                    turn, at = divmod(u - 1, UNITS)
                    for kind, t in misc_at(i + turn, at):
                        if kind == "ot":
                            row = (i + turn) * ROWS + (t if at >= OT_AT else t - ROWS)
                            dve.wait_ge(oT_hi_ready, row + 1)
                            vec.tensor_tensor(oT_lo[:].rearrange("p r (w c) -> p w r c", c=WIN),
                                              misc_ps[:].rearrange("p (w n) -> p w n", n=ODD)[:, :, 0:N]
                                              .rearrange("p w (r c) -> p w r c", c=WIN),
                                              oT_hi[:].rearrange("p r (w c) -> p w r c", c=WIN), ALU.subtract)\
                                .then_inc(misc_free, 1)
                    if live(i):
                        g = i * UNITS + u
                        dve.wait_ge(scores_ready, g + 1)
                        need(dve, probs_ready, g - 3)
                        edge = int(u // PAIRS == ROWS - 1)
                        vec.tensor_tensor(s_sb[0:QP, u % 4].rearrange("p w h m -> p (w h m)"),
                                          scores_ps[0:QP, u % 2, 0:WP * 2 * N],
                                          bias[0:QP, edge, u % PAIRS].rearrange("p w h m -> p (w h m)"), ALU.add)\
                            .then_inc(biased, 1)
                        dve.wait_ge(biased, g + 1)
                        vec.tensor_reduce(s_max[0:QP, u % 4], s_sb[0:QP, u % 4].rearrange("p w h m -> p (w h) m"),
                                          AX.X, ALU.max).then_inc(max_ready, 1)
                    t, half = divmod(u - VLO_AT, 2)
                    if 0 <= t < TILES and live(i, -1):
                        dve.wait_ge(plane_hi_ready, ((i - 1) * TILES + t) * 2 + half + 1)
                        two, at = slice(2 * half, 2 * half + 2), slice(t * TPAIRS, (t + 1) * TPAIRS)
                        vec.tensor_tensor(plane_lo[:, two, at, 1:W + 1], plane[:, t % 2, two],
                                          plane_hi[:, two, at, 1:W + 1], ALU.subtract).then_inc(plane_lo_ready, 1)
                    if u in XC_AT and live(i, -1):
                        t0, t1 = XC_AT[u]
                        need(dve, conv_out, (i - 2) * TILES + t1)
                        vec.tensor_copy(flat(x_c)[:, t0 * TP:t1 * TP], flat(x_b)[:, t0 * TP:t1 * TP]).then_inc(xc_ready, 1)
                    for t in range(TILES):
                        turn, at = half_done(t)
                        if u == at and live(i, -1 - turn):
                            number = (i - 1 - turn) * TILES + t
                            dve.wait_ge(m1_ready, number + 1)
                            need(dve, conv_sums, number * 4)
                            vec.tensor_tensor(m_sum[:], m_1[:], conv_ps[:, 0, 0:PP], ALU.add).then_inc(conv_sums, 1)
                    for kind, t in misc_at(i, u - 1):
                        if kind == "tin":
                            dve.wait_ge(misc_free, misc_number(i, kind, t) + 1)
                            vec.bn_stats(gn1.stats[:, t, :], flat(x_a)[:, t * TP:(t + 1) * TP]).then_inc(gn1.stat, 1)
                            if t == TILES - 1:
                                norm_first(gn1, i + 1)
                    for kind, t in misc_at(i, u):
                        number = misc_number(i, kind, t)
                        if kind == "proj":
                            dve.wait_ge(misc_ready, number + 1)
                            if t == 0:
                                dve.wait_ge(xa_free, (i + 1) * len(XB_AT) - 1)
                            if t == ROWS - 2:
                                dve.wait_ge(xa_free, i * len(XB_AT))
                            pieces = list(roll_pieces(WIN, t * WIN))
                            proj = misc_ps[:, 0:RT].rearrange("p (r w) -> p r w", w=W)
                            for rows, cols, y0, x0 in pieces:
                                n, m = rows.stop - rows.start, cols.stop - cols.start
                                at = x_b[:, y0:y0 + n, x0:x0 + m]
                                last = vec.scalar_tensor_tensor(out=at, in0=proj[:, rows, cols], scalar=w_max[:, 3:4],
                                                                in1=at, op0=ALU.mult, op1=ALU.add)
                            last.then_inc(misc_free, 1)
                            dve.wait_ge(misc_free, number + 1)
                            spans = sorted({(y0, rows.stop - rows.start) for rows, _, y0, _ in pieces}, reverse=True)
                            for n, (y0, height) in enumerate(spans):
                                vec.bn_stats(gn2.stats[:, t + n, :], flat(x_b)[:, y0 * W:(y0 + height) * W])\
                                    .then_inc(gn2.stat, 1)
                            if t == ROWS - 1:
                                norm_first(gn2, i - 1)
                        if kind in ("gn1", "gn2"):
                            gn, img = (gn1, i + 1) if kind == "gn1" else (gn2, i - 1)
                            if t == 0:
                                norm_second(gn, img, number)
                            else:
                                norm_third(gn, img, number, norm_steps)
                    for t in range(TILES):
                        turn, at = tile_done(t)
                        if u == at and live(i, -1 - turn):
                            img = i - 1 - turn
                            number = img * TILES + t
                            m = [conv_ps[:, j, 0:PP] for j in range(PLANES)]
                            y = [conv_y[:, :, odd, :] for odd in range(2)]
                            dve.wait_ge(conv_ready, number + 1)
                            dve.wait_ge(conv_sums, number * 4 + 1)
                            need(dve, conv_out, number)
                            vec.tensor_tensor(m_diff[:], m_1[:], m[2], ALU.subtract).then_inc(conv_sums, 1)
                            vec.tensor_tensor(y[0], m[2].rearrange("p (r w) -> p r w", w=W),
                                              m_sum[:].rearrange("p (r w) -> p r w", w=W), ALU.add).then_inc(conv_sums, 1)
                            dve.wait_ge(conv_sums, number * 4 + 2)
                            vec.tensor_tensor(y[1], m_diff[:].rearrange("p (r w) -> p r w", w=W),
                                              m[3].rearrange("p (r w) -> p r w", w=W), ALU.subtract).then_inc(conv_sums, 1)
                            dve.wait_ge(conv_sums, number * 4 + 4)
                            dve.wait_ge(xc_ready, (img + 1) * len(XC_AT))
                            if t > 0 or not isinstance(img, int) or img > 0:
                                before = i - turn + (tile_turned(t - 1)[0] if t > 0 else tile_turned(TILES - 1)[0] - 1)
                                dve.wait_ge(misc_ready, misc_number(before, "tout", (t - 1) % TILES) + 1)
                            vec.scalar_tensor_tensor(out=result[:], in0=conv_y[:].rearrange("p r a w -> p (r a w)"),
                                                     scalar=wc_scale[:], in1=flat(x_c)[:, t * TP:(t + 1) * TP],
                                                     op0=ALU.mult, op1=ALU.add).then_inc(conv_out, 1)
                    turn, row = divmod(u - LO_AT, UNITS)
                    if row < ROWS and live(i, 1 + turn):
                        dve.wait_ge(tok_hi_ready, (i + 1 + turn) * ROWS + row + 1)
                        at = slice(row * NWIN, (row + 1) * NWIN)
                        vec.tensor_tensor(
                            tok_lo[:, at, 0:N].rearrange("p w (r c) -> p w r c", c=WIN),
                            x_n[:, 1 + row * WIN:1 + (row + 1) * WIN, :].rearrange("p r (w c) -> p w r c", c=WIN),
                            tok_hi[:, at, 0:N].rearrange("p w (r c) -> p w r c", c=WIN), ALU.subtract)\
                            .then_inc(tok_lo_ready, 1)

            def channel_scales():
                dve.wait_ge(setup_pe, 5)
                step(vec.tensor_copy(wc_scale[:], conv_ps[:, 0, 0:1]))

            over_images(dve, body, channel_scales)

        @block.tensor
        def _(pe):
            mm = nc.tensor.matmul
            pe.wait_ge(const_in, 16 * N_CONST)
            pe.wait_ge(tap_sums, 1)
            mm(misc_ps[:, 0:C], ones, wc_sum, start=True, stop=True).then_inc(setup_pe, 1)
            pe.wait_ge(qkv_scaled, 1)
            for t in range(3):
                nc.tensor.transpose(misc_ps[:, t * C:(t + 1) * C], w_f[:, t, :], ident[:])
            nc.tensor.transpose(misc_ps[:, 3 * C:4 * C], w_in[:, 3, :], ident[:]).then_inc(setup_pe, 1)
            pe.wait_ge(proj_turned, 1)
            nc.tensor.transpose(misc_ps[:, 0:C], w_f[:, 3, :], ident[:])
            mm(misc_ps[:, C:C + 2], w_in[:, 3, :], bv2[:], start=True, stop=True).then_inc(setup_pe, 1)
            pe.wait_ge(proj_scaled, 1)
            nc.tensor.transpose(misc_ps[:, 0:C], w_in[:, 3, :], ident[:]).then_inc(setup_pe, 1)
            pe.wait_ge(scales_ready, 1)

            def three(out_ps, pairs_of_parts):
                for n, (w, t) in enumerate(pairs_of_parts):
                    last = mm(out_ps, w, t, start=(n == 0), stop=(n == 2))
                return last

            def scores(i, u):
                g, (r, pair) = i * UNITS + u, divmod(u, PAIRS)
                if pair == 0:
                    pe.wait_ge(qkv_free, (i * ROWS + r) * 4 + 2)
                need(pe, biased, g)
                for w in range(NWIN):
                    for n in range(2):
                        p0, at = ODD * (w % 2), slice((pair + n) * 32, (pair + n) * 32 + 32)
                        last = mm(scores_ps[p0:p0 + N, (u + n) % 2, (w // 2) * 2 * N:(w // 2 + 1) * 2 * N],
                                  q[at, r % 2, w, :], k[at, r % 2, w].rearrange("p e m -> p (e m)"),
                                  start=True, stop=True)
                        if w == NWIN - 1:
                            last.then_inc(scores_ready, 1)

            def turn_probs(i, u):
                g = i * UNITS + u
                pe.wait_ge(probs_ready, g + 1)
                need(pe, probsT_sb, g)
                for w in range(WP):
                    last = nc.tensor.transpose(probsT_ps[:, w * 128:w * 128 + QP],
                                               probs[0:QP, u % 2, w].rearrange("p e m -> p (e m)"), ident[0:QP, 0:QP])
                last.then_inc(probsT_ready, 1)

            def values(i, u):
                g, (r, pair) = i * UNITS + u, divmod(u, PAIRS)
                pe.wait_ge(probsT_sb, g + 1)
                if pair == 0:
                    pe.wait_ge(qkv_free, (i * ROWS + r) * 4 + 4)
                if pair % 2 == 0:
                    need(pe, attn_norm, (i * ROWS + r) * 2 + pair // 2)
                for w in range(NWIN):
                    p0, wp = ODD * (w % 2), w // 2
                    at = (wp * 2 + pair % 2) * VW
                    last = mm(attn_ps[p0:p0 + N, at:at + VW], probsT[:, u % 2, w, :], v[:, r % 2, w, pair, :],
                              start=True, stop=True)
                last.then_inc(attn_ready, 1)

            def qkv(i, u):
                r, j = divmod(u, PAIRS)
                row = (r + 1) % ROWS
                number = (i * ROWS + (r + 1)) * 4 + j
                need(pe, qkv_free, number)
                if j == 0:
                    pe.wait_ge(tok_lo_ready, i * ROWS + (r + 1) + 1)
                wins = slice(row * NWIN, (row + 1) * NWIN)
                if j < 2:
                    hi, lo = tok_hi[:, wins, 0:N], tok_lo[:, wins, 0:N]
                    last = three(qkv_ps[:, 0:RT].rearrange("p (w n) -> p w n", n=N),
                                 ((wT_hi[:, j, :], hi), (wT_hi[:, j, :], lo), (wT_lo[:, j, :], hi)))
                else:
                    runs = [(b * C, slice(0, 128), (j - 2) * 4 + b) for b in range(4)]
                    if j == 3:
                        runs[3:] = [(3 * C, slice(0, ODD), NWIN - 1), (3 * C, slice(ODD, 128), 0)]
                    for col, parts, w in runs:
                        at, width = (row * NWIN + w) * ODD, parts.stop - parts.start
                        hi, lo = (t[:].rearrange("p w n -> p (w n)")[:, at:at + width] for t in (tok_hi, tok_lo))
                        last = three(qkv_ps[parts, col:col + C],
                                     ((hi, wT_hi[:, 2, :]), (lo, wT_hi[:, 2, :]), (hi, wT_lo[:, 2, :])))
                last.then_inc(qkv_ready, 1)

            def misc(i, u, kind, t):
                number = misc_number(i, kind, t)
                need(pe, misc_free, number)
                if kind == "tin":
                    pe.wait_ge(x_loaded[t], (i + 2) * 16)
                    for s in range(SUB):
                        last = nc.tensor.transpose(misc_ps[:, s * 128:s * 128 + SP_], x_in[:, t * SUB + s, :],
                                                   ident[0:SP_, 0:SP_])
                if kind == "tout":
                    img = i - 1 - tile_turned(t)[0]
                    pe.wait_ge(conv_out, img * TILES + t + 1)
                    for s in range(SUB):
                        last = nc.tensor.transpose(misc_ps[0:SP_, s * C:(s + 1) * C], result[:, s * SP_:(s + 1) * SP_], ident[:])
                if kind == "ot":
                    pe.wait_ge(attn_norm, (i * ROWS + (t + 1 if u >= OT_AT else t + 1 - ROWS)) * 2)
                    for w in range(WP):
                        last = nc.tensor.transpose(misc_ps[:, w * 128:w * 128 + QP], o_sb[0:QP, w, :], ident[0:QP, 0:QP])
                if kind == "proj":
                    hi, lo = (o[:].rearrange("p r w -> p (r w)") for o in (oT_hi, oT_lo))
                    last = three(misc_ps[:, 0:RT], ((wT_hi[:, 3, :], hi), (wT_hi[:, 3, :], lo), (wT_lo[:, 3, :], hi)))
                if kind in ("gn1", "gn2"):
                    gn, img = (gn1, i + 1) if kind == "gn1" else (gn2, i - 1)
                    if t == 0:
                        pe.wait_ge(gn.mv_ready, img + 1)
                    else:
                        pe.wait_ge(gn.var_ready, (img + 1) * 3)
                    last = mm(misc_ps[:, 0:2], group[:], gn.mv[:] if t == 0 else gn.var[:], start=True, stop=True)
                last.then_inc(misc_ready, 1)

            def conv(i, u, place):
                turn = 0 if u >= CONV_AT else 1
                k, at = divmod(u + turn * UNITS - CONV_AT, CONV_STEPS)
                img = i - 1 - turn
                if k >= TILES or not live(img):
                    return
                first = sum(map(sum, CONV_PARTS[:at])) + sum(CONV_PARTS[at][:place])
                for n in range(first, first + CONV_PARTS[at][place]):
                    j, (part, dx) = PLANE_ORDER[n // (3 * KW)], divmod(n % (3 * KW), KW)
                    if n == 0:
                        need(pe, conv_sums, (img * TILES + k) * 4)
                    half, rest = divmod(n, 2 * 3 * KW)
                    if rest == 0:
                        pe.wait_ge(plane_hi_ready, (img * TILES + k) * 2 + half + 1)
                    if rest == 2 * KW:
                        pe.wait_ge(plane_lo_ready, (img * TILES + k) * 2 + half + 1)
                    w, p = ((wc_hi, plane_hi), (wc_lo, plane_hi), (wc_hi, plane_lo))[part]
                    last = mm(conv_ps[:, j, 0:PP].rearrange("p (r w) -> p r w", w=W), w[:, j * KW + dx, :],
                              p[:, j, k * TPAIRS:(k + 1) * TPAIRS, dx:dx + W],
                              start=(n % (3 * KW) == 0), stop=(n % (3 * KW) == 3 * KW - 1))
                    if n == 2 * 3 * KW - 1:
                        last.then_inc(conv_half, 1)
                    if n == PLANES * 3 * KW - 1:
                        last.then_inc(conv_ready, 1)

            def body(i):
                for u in range(UNITS):
                    if u % 2 == 0 and live(i):
                        scores(i, u)
                    conv(i, u, 0)
                    if live(i, 0 if u >= LAG_T else -1):
                        turn_probs(i if u >= LAG_T else i - 1, (u - LAG_T) % UNITS)
                    for job in misc_at(i, u, (MID,)):
                        misc(i, u, *job)
                    conv(i, u, 1)
                    late = (u - LAG_PV) % 2 == 0
                    have_values = live(i, 0 if u >= LAG_PV else -1)
                    if have_values and not late:
                        values(i if u >= LAG_PV else i - 1, (u - LAG_PV) % UNITS)
                    if live(i, 0 if u // PAIRS < ROWS - 1 else 1):
                        qkv(i, u)
                    if have_values and late:
                        values(i if u >= LAG_PV else i - 1, (u - LAG_PV) % UNITS)
                    conv(i, u, 2)
                    for job in misc_at(i, u, (END,)):
                        misc(i, u, *job)

            def channel_scales():
                pe.wait_ge(setup_done, 1)
                nc.tensor.transpose(conv_ps[:, 0, 0:C], wc_chmax, ident[:]).then_inc(setup_pe, 1)

            over_images(pe, body, channel_scales)


N_CONST = 12 + 2 * WIN


_INS = ["x", "L0_conv_qkv_weight", "L0_conv_qkv_bias", "L0_conv_proj_weight", "L0_conv_proj_bias",
        "L0_conv_rel_pos_table", "L1_conv_w", "L1_conv_pruning_mask"]


def _constants():
    import numpy as np

    c = np.arange(C)
    ident = np.eye(C, dtype=np.float32)
    group = (c[:, None] // 4 == c[None, :] // 4).astype(np.float32) / 4
    parity = np.stack([(c // HD) % 2 == e for e in range(2)], axis=1).astype(np.float32)
    side = np.zeros((H, W))
    cuts = ((0, H - WIN), (H - WIN, H - SHIFT), (H - SHIFT, H))
    for a, (y0, y1) in enumerate(cuts):
        for b, (x0, x1) in enumerate(cuts):
            side[y0:y1, x0:x1] = 3 * a + b
    mask = np.zeros((128, 2, WP, N), np.float32)
    for a, row in enumerate((0, ROWS - 1)):
        for w in range(NWIN):
            s = side[row * WIN:(row + 1) * WIN, w * WIN:(w + 1) * WIN].reshape(-1)
            p0 = ODD * (w % 2)
            mask[p0:p0 + N, a, w // 2] = np.where(s[:, None] != s[None, :], -100.0, 0.0)
    return {"ident": ident, "group": group, "parity": parity, "mask": mask}


def kernel(**inputs):
    import numpy as _np
    import concourse.bacc as _bacc
    from concourse import mybir as _mybir
    from concourse.bass_utils import run_bass_kernel_spmd as _run

    nc = _bacc.Bacc("TRN2", target_bir_lowering=False, num_devices=1)
    arrays, args = {}, []
    for name, a in [(n, inputs[n]) for n in _INS] + list(_constants().items()):
        a = _np.ascontiguousarray(a)
        arrays[f"in_{name}_dram"] = a
        args.append(nc.dram_tensor(f"in_{name}_dram", a.shape, _mybir.dt.from_np(a.dtype), kind="ExternalInput").ap())
    args.append(nc.dram_tensor("out_0_dram", (IMGS, H, W, C), F32, kind="ExternalOutput").ap())
    build_block(nc, *args)
    r = _run(nc, [arrays], core_ids=[0])
    return r.results[0]["out_0_dram"]
```
